# Optimizing a Trainium2 kernel written in Bass

```python
import numpy as np
import jax
import jax.numpy as jnp

def _softmax(x, axis=-1):
    return jax.nn.softmax(x, axis=axis)

def _gelu(x):
    return jax.nn.gelu(x, approximate=True)

def _silu(x):
    return jax.nn.silu(x)

def _sigmoid(x):
    return jax.nn.sigmoid(x)

def _layernorm(x, axis=-1, eps=1e-05):
    m = jnp.mean(x, axis=axis, keepdims=True)
    v = jnp.var(x, axis=axis, keepdims=True)
    return (x - m) / jnp.sqrt(v + eps)

def _scatter_add(tgt, idx, src, axis=0):
    return tgt.at[idx].add(src)

def _segment_sum(src, seg, n):
    return jax.ops.segment_sum(src, seg, n)
kernel_name = 'mk_prb_d2_jaxref_r8_2739e7'

def setup_inputs(seed: int=0):
    np.random.seed(seed)
    _w = jnp.asarray

    def _L0_attn_setup():
        import jax, jax.numpy as jnp
        import numpy as np
        B, S, H = (4, 256, 256)
        key = jax.random.key(seed)
        k1, k2, k3 = jax.random.split(key, 3)
        xav_qkv = float(np.sqrt(6.0 / (H + 3 * H)))
        xav_out = float(np.sqrt(6.0 / (H + H)))
        return {'hidden_states': jax.random.normal(k1, (B, S, H), dtype=jnp.float32), 'w_qkv': jax.random.uniform(k2, (3 * H, H), minval=-xav_qkv, maxval=xav_qkv, dtype=jnp.float32), 'b_qkv': jnp.zeros((3 * H,), dtype=jnp.float32), 'w_out': jax.random.uniform(k3, (H, H), minval=-xav_out, maxval=xav_out, dtype=jnp.float32), 'b_out': jnp.zeros((H,), dtype=jnp.float32)}
    _L0_attn_in = _L0_attn_setup()

    def _L0_ffn_setup():
        import jax, jax.numpy as jnp
        import numpy as np
        TOP_K = 4
        key = jax.random.key(seed)
        ks = jax.random.split(key, 8)
        B, S, H, E, F = (1, 256, 256, 16, 176)
        Fs = 2 * F
        s = 0.02
        return {'hidden_states': jax.random.normal(ks[0], (B, S, H), jnp.float32), 'gate_weight': jax.random.normal(ks[1], (E, H), jnp.float32) * s, 'w_gate': jax.random.normal(ks[2], (E, H, F), jnp.float32) * s, 'w_up': jax.random.normal(ks[3], (E, H, F), jnp.float32) * s, 'w_down': jax.random.normal(ks[4], (E, F, H), jnp.float32) * s, 'ws_gate': jax.random.normal(ks[5], (H, Fs), jnp.float32) * s, 'ws_up': jax.random.normal(ks[6], (H, Fs), jnp.float32) * s, 'ws_down': jax.random.normal(ks[7], (Fs, H), jnp.float32) * s}
    _L0_ffn_in = _L0_ffn_setup()

    def _L1_attn_setup():
        import math
        import jax, jax.numpy as jnp
        import numpy as np
        MODEL_DIM = 256
        N_HEADS = 32
        N_GROUPS = 8
        R = N_HEADS // N_GROUPS
        HEAD_DIM = MODEL_DIM // N_HEADS
        KV_DIM = MODEL_DIM // R
        B, S = (1, 256)
        key = jax.random.key(seed)
        k1, k2, k3 = jax.random.split(key, 3)
        scale = 0.02
        return {'x': jax.random.normal(k1, (B, S, MODEL_DIM), dtype=jnp.float32), 'w_qkv': jax.random.normal(k2, (MODEL_DIM + 2 * KV_DIM, MODEL_DIM), dtype=jnp.float32) * scale, 'b_qkv': jnp.zeros((MODEL_DIM + 2 * KV_DIM,), dtype=jnp.float32), 'w_out': jax.random.normal(k3, (MODEL_DIM, MODEL_DIM), dtype=jnp.float32) * scale, 'b_out': jnp.zeros((MODEL_DIM,), dtype=jnp.float32)}
    _L1_attn_in = _L1_attn_setup()

    def _L1_ffn_setup():
        import jax, jax.numpy as jnp
        import numpy as np
        NUM_ROUTED = 7
        TOP_K = 3
        D = 256
        H = 256
        B, S = (4, 256)

        def _expert_ffn(x, w1, wg, w2):
            return jax.nn.silu(x @ w1) * (x @ wg) @ w2
        key = jax.random.key(seed)
        ks = jax.random.split(key, 8)
        s = 0.02
        return {'x': jax.random.normal(ks[0], (B, S, D), jnp.float32), 'W1': jax.random.normal(ks[1], (NUM_ROUTED, D, H), jnp.float32) * s, 'Wg': jax.random.normal(ks[2], (NUM_ROUTED, D, H), jnp.float32) * s, 'W2': jax.random.normal(ks[3], (NUM_ROUTED, H, D), jnp.float32) * s, 'Ws1': jax.random.normal(ks[4], (D, H), jnp.float32) * s, 'Wsg': jax.random.normal(ks[5], (D, H), jnp.float32) * s, 'Ws2': jax.random.normal(ks[6], (H, D), jnp.float32) * s, 'gate_w': jax.random.normal(ks[7], (D, NUM_ROUTED), jnp.float32) * s, 'gate_b': jnp.zeros((NUM_ROUTED,), jnp.float32), 'biases': jnp.zeros((NUM_ROUTED,), jnp.float32)}
    _L1_ffn_in = _L1_ffn_setup()
    _d = {'L0_attn_hidden_states': _L0_attn_in['hidden_states'], 'L0_attn_w_qkv': _L0_attn_in['w_qkv'], 'L0_attn_b_qkv': _L0_attn_in['b_qkv'], 'L0_attn_w_out': _L0_attn_in['w_out'], 'L0_attn_b_out': _L0_attn_in['b_out'], 'L0_ffn_gate_weight': _L0_ffn_in['gate_weight'], 'L0_ffn_w_gate': _L0_ffn_in['w_gate'], 'L0_ffn_w_up': _L0_ffn_in['w_up'], 'L0_ffn_w_down': _L0_ffn_in['w_down'], 'L0_ffn_ws_gate': _L0_ffn_in['ws_gate'], 'L0_ffn_ws_up': _L0_ffn_in['ws_up'], 'L0_ffn_ws_down': _L0_ffn_in['ws_down'], 'L1_attn_w_qkv': _L1_attn_in['w_qkv'], 'L1_attn_b_qkv': _L1_attn_in['b_qkv'], 'L1_attn_w_out': _L1_attn_in['w_out'], 'L1_attn_b_out': _L1_attn_in['b_out'], 'L1_ffn_W1': _L1_ffn_in['W1'], 'L1_ffn_Wg': _L1_ffn_in['Wg'], 'L1_ffn_W2': _L1_ffn_in['W2'], 'L1_ffn_Ws1': _L1_ffn_in['Ws1'], 'L1_ffn_Wsg': _L1_ffn_in['Wsg'], 'L1_ffn_Ws2': _L1_ffn_in['Ws2'], 'L1_ffn_gate_w': _L1_ffn_in['gate_w'], 'L1_ffn_gate_b': _L1_ffn_in['gate_b'], 'L1_ffn_biases': _L1_ffn_in['biases']}
    _x0 = _d['L0_attn_hidden_states']
    _d['L0_attn_hidden_states'] = jax.random.normal(jax.random.fold_in(jax.random.key(seed), 1), (4, 512, 256), dtype=_x0.dtype)
    del _x0
    return _d

def reference(L0_attn_hidden_states, L0_attn_w_qkv, L0_attn_b_qkv, L0_attn_w_out, L0_attn_b_out, L0_ffn_gate_weight, L0_ffn_w_gate, L0_ffn_w_up, L0_ffn_w_down, L0_ffn_ws_gate, L0_ffn_ws_up, L0_ffn_ws_down, L1_attn_w_qkv, L1_attn_b_qkv, L1_attn_w_out, L1_attn_b_out, L1_ffn_W1, L1_ffn_Wg, L1_ffn_W2, L1_ffn_Ws1, L1_ffn_Wsg, L1_ffn_Ws2, L1_ffn_gate_w, L1_ffn_gate_b, L1_ffn_biases):

    def _L0_attn_ref(hidden_states, w_qkv, b_qkv, w_out, b_out):
        import jax, jax.numpy as jnp
        import numpy as np
        B, S, H = (4, 256, 256)
        Bc, Sc, Hc = hidden_states.shape
        scaling = jnp.sqrt(jnp.asarray(Hc, hidden_states.dtype))
        qkv = jnp.einsum('bsh,oh->bso', hidden_states, w_qkv) + b_qkv
        q, k, v = jnp.split(qkv, 3, axis=-1)
        scores = jnp.einsum('bqh,bkh->bqk', q, k) / scaling
        probs = jax.nn.softmax(scores, axis=-1)
        context = jnp.einsum('bqk,bkh->bqh', probs, v)
        out = jnp.einsum('bsh,oh->bso', context, w_out) + b_out
        return out

    def _L0_ffn_ref(hidden_states, gate_weight, w_gate, w_up, w_down, ws_gate, ws_up, ws_down):
        import jax, jax.numpy as jnp
        import numpy as np
        TOP_K = 4
        B, S, H = hidden_states.shape
        E = gate_weight.shape[0]
        x = hidden_states.reshape(-1, H)
        T = x.shape[0]
        logits = jnp.einsum('th,eh->te', x.astype(jnp.float32), gate_weight.astype(jnp.float32))
        probs = jax.nn.softmax(logits, axis=1)
        top_vals, top_idx = jax.lax.top_k(probs, TOP_K)
        dense_w = jnp.zeros((T, E), probs.dtype).at[jnp.arange(T)[:, None], top_idx].add(top_vals)
        g = jnp.einsum('th,ehf->tef', x, w_gate)
        u = jnp.einsum('th,ehf->tef', x, w_up)
        a = jax.nn.silu(g) * u
        routed = jnp.einsum('te,tef,efh->th', dense_w.astype(x.dtype), a, w_down)
        shared = jnp.einsum('tf,fh->th', jax.nn.silu(x @ ws_gate) * (x @ ws_up), ws_down)
        out = (routed + shared).reshape(B, S, H)
        return out

    def _L1_attn_ref(x, w_qkv, b_qkv, w_out, b_out):
        import math
        import jax, jax.numpy as jnp
        import numpy as np
        MODEL_DIM = 256
        N_HEADS = 32
        N_GROUPS = 8
        R = N_HEADS // N_GROUPS
        HEAD_DIM = MODEL_DIM // N_HEADS
        KV_DIM = MODEL_DIM // R
        B, S = (1, 256)
        Bx, Sx, _ = x.shape
        fused = x @ w_qkv.T + b_qkv
        q = fused[..., :MODEL_DIM]
        k = fused[..., MODEL_DIM:MODEL_DIM + KV_DIM]
        v = fused[..., MODEL_DIM + KV_DIM:]
        q = q.reshape(Bx, Sx, N_GROUPS, R, HEAD_DIM).transpose(0, 2, 3, 1, 4)
        k = k.reshape(Bx, Sx, N_GROUPS, HEAD_DIM).transpose(0, 2, 1, 3)
        v = v.reshape(Bx, Sx, N_GROUPS, HEAD_DIM).transpose(0, 2, 1, 3)
        sim = jnp.einsum('bgrsd,bgtd->bgrst', q, k) / math.sqrt(HEAD_DIM)
        attn = jax.nn.softmax(sim, axis=-1)
        out = jnp.einsum('bgrst,bgtd->bgrsd', attn, v)
        out = out.transpose(0, 3, 1, 2, 4).reshape(Bx, Sx, MODEL_DIM)
        return out @ w_out.T + b_out

    def _L1_ffn_ref(x, W1, Wg, W2, Ws1, Wsg, Ws2, gate_w, gate_b, biases):
        import jax, jax.numpy as jnp
        import numpy as np
        NUM_ROUTED = 7
        TOP_K = 3
        D = 256
        H = 256
        B, S = (4, 256)

        def _expert_ffn(x, w1, wg, w2):
            return jax.nn.silu(x @ w1) * (x @ wg) @ w2
        output = _expert_ffn(x, Ws1, Wsg, Ws2)
        gate_logits = x @ gate_w + gate_b
        gate_probas = jax.nn.softmax(gate_logits, axis=-1)
        biased_probas = gate_probas + biases
        _, topk_idxs = jax.lax.top_k(biased_probas, TOP_K)
        topk_probas = jnp.take_along_axis(gate_probas, topk_idxs, axis=-1)
        topk_probas = topk_probas / jnp.sum(topk_probas, axis=-1, keepdims=True)
        for e in range(NUM_ROUTED):
            w_e = jnp.sum(topk_probas * (topk_idxs == e), axis=-1)
            output = output + _expert_ffn(x, W1[e], Wg[e], W2[e]) * w_e[..., None]
        return output
    x = L0_attn_hidden_states
    xn = _layernorm(x, axis=-1)
    x = x + _L0_attn_ref(xn, L0_attn_w_qkv, L0_attn_b_qkv, L0_attn_w_out, L0_attn_b_out) + _L0_ffn_ref(xn, L0_ffn_gate_weight, L0_ffn_w_gate, L0_ffn_w_up, L0_ffn_w_down, L0_ffn_ws_gate, L0_ffn_ws_up, L0_ffn_ws_down)
    xn = _layernorm(x, axis=-1)
    x = x + _L1_attn_ref(xn, L1_attn_w_qkv, L1_attn_b_qkv, L1_attn_w_out, L1_attn_b_out) + _L1_ffn_ref(xn, L1_ffn_W1, L1_ffn_Wg, L1_ffn_W2, L1_ffn_Ws1, L1_ffn_Wsg, L1_ffn_Ws2, L1_ffn_gate_w, L1_ffn_gate_b, L1_ffn_biases)
    return x

_drawn_inputs = setup_inputs


def setup_inputs(seed=0):
    import zlib

    import numpy as np

    out = dict(_drawn_inputs(seed))
    spreads = {'L0_attn_b_qkv': (0.0, 0.1),
     'L0_attn_b_out': (0.0, 0.1),
     'L1_attn_b_qkv': (0.0, 1.817),
     'L1_attn_b_out': (0.0, 0.591),
     'L1_ffn_gate_b': (0.0, 0.8),
     'L1_ffn_biases': (0.0, 0.8)}
    factors = {'L0_ffn_gate_weight': 8.0,
     'L0_ffn_w_gate': 8.0,
     'L0_ffn_w_up': 8.0,
     'L0_ffn_w_down': 8.0,
     'L0_ffn_ws_gate': 2.97,
     'L0_ffn_ws_up': 2.939,
     'L0_ffn_ws_down': 2.932,
     'L1_attn_w_qkv': 17.948,
     'L1_ffn_W1': 5.845,
     'L1_ffn_Wg': 5.753,
     'L1_ffn_W2': 5.754,
     'L1_ffn_Ws1': 3.45,
     'L1_ffn_Wsg': 3.402,
     'L1_ffn_Ws2': 3.412,
     'L1_ffn_gate_w': 8.0,
     'L1_attn_w_out': 3.074}
    for name, (base, spread) in spreads.items():
        noise = np.random.default_rng([zlib.crc32(name.encode()), seed]).standard_normal(out[name].shape)
        drawn = base * np.exp(spread * noise) if base else spread * noise
        out[name] = jnp.asarray(drawn.astype(out[name].dtype))
    for name, factor in factors.items():
        out[name] = (out[name] * factor).astype(out[name].dtype)
    return out
```

```python
import concourse.bass as bass
from concourse import mybir
from contextlib import ExitStack

P = 128
B, S, H = 4, 512, 256
T = B * S
TT = T // P
KH = H // P
QT = S // P
E0, TOP0, F0, FS0 = 16, 4, 176, 352
E1, TOP1, F1 = 7, 3, 256
NF0, G0 = 5, 5
NF1, G1 = 4, 4
WC = 2 * H + 2 * P + 0 + 0
WC = 2 * KH * P
WT = WC + H
WS = WT + P
NG, R, HD = 8, 4, 8
EPS = 1e-5
LN_COLS = 2 * (E0 + 1)
LN_COLS1 = 2 * (E1 + 1)
AW0 = KH * 3 * H + KH * H + KH * E0
AW1 = KH * (H + 2 * NG * HD) + KH * H + KH * (E1 + 1)
NSELQ = 2 * 4 * P
NSELK = 2 * NG * P
CF = P + 1 + E0 * E0 + E1 * E1
BF = 6 + 2 + 3 + 2 + 2 * E1


def program(nc, x_in, aw0_in, aw1_in, sel_in, ffn0_in, ffn1_in, const_in, bias_in, out):
    f32, f32r = mybir.dt.float32, mybir.dt.float32r
    ALU, ACT, AX = mybir.AluOpType, mybir.ActivationFunctionType, mybir.AxisListType
    ctx = ExitStack()
    with ctx:
        def sb(name, shape, dt=f32):
            return ctx.enter_context(nc.sbuf_tensor(name, shape, dt))

        def sem(name):
            return ctx.enter_context(nc.semaphore(name))

        x = sb("x", [P, TT, H])
        yacc = sb("yacc", [P, KH, T])
        xn = yacc[:].rearrange("p k t -> p (k t)").rearrange("p (t h) -> p t h", h=H)
        xt_hi = sb("xt_hi", [P, KH, T], f32r)
        xt_lo = sb("xt_lo", [P, KH, T], f32r)
        wt = sb("wt", [P, T], f32r)
        raw = sb("raw", [P, NF0 * WS])
        awr = sb("awr", [P, max(2 * AW0, 2 * AW1 + NSELQ + NSELK)], f32r)
        const = sb("const", [P, CF])
        bias = sb("bias", [P, BF])
        st = sb("st", [P, TT, 6])
        mv = sb("mv", [P, TT, 2])
        rs = sb("rs", [P, 8, TT])
        lg = sb("lg", [P, TT, E0])
        pr = sb("pr", [P, TT, E0])
        rank = sb("rank", [P, TT, E0])
        gw = sb("gw", [P, TT * LN_COLS + P], f32r)
        work_r = sb("work_r", [P, 12416], f32r)
        work_f = sb("work_f", [P, 7680])

        bank = [ctx.enter_context(nc.psum_tensor(f"bank{i}", [P, 512], f32)) for i in range(0)]
        psum = ctx.enter_context(nc.psum_tensor("psum", [P, 8, 512], f32))

        ident = const[:, 0:P]
        kone = const[:, P:P + 1]
        low0 = const[:, P + 1:P + 1 + E0 * E0]
        low1 = const[:, P + 1 + E0 * E0:CF]
        bq0, bo0, bq1, bo1 = bias[:, 0:6], bias[:, 6:8], bias[:, 8:11], bias[:, 11:13]
        gate_b, route_b = bias[:, 13:13 + E1], bias[:, 13 + E1:13 + 2 * E1]

        def carve(tensor):
            at = [0]

            def take(*shape):
                n = 1
                for s in shape:
                    n *= s
                ap = tensor[:, at[0]:at[0] + n]
                at[0] += n
                if len(shape) == 2:
                    ap = ap.rearrange("p (a b) -> p a b", b=shape[1])
                if len(shape) == 3:
                    ap = ap.rearrange("p (a b c) -> p a b c", b=shape[1], c=shape[2])
                return ap
            return take

        def attention_weights(aw, nq, ng):
            take = carve(awr)
            a = [take(aw), take(aw)]
            nqk = KH * nq
            return [(w[:, 0:nqk].rearrange("p (k n) -> p k n", k=KH),
                     w[:, nqk:nqk + KH * H].rearrange("p (k n) -> p k n", k=KH),
                     w[:, nqk + KH * H:aw].rearrange("p (k n) -> p k n", k=KH)) for w in a], take
        (w0_hi, w0_lo), _ = attention_weights(AW0, 3 * H, E0)
        (w1_hi, w1_lo), take = attention_weights(AW1, H + 2 * NG * HD, E1 + 1)
        selq = take(2, 4, P)
        selk = take(2, NG, P)

        tr, tf = carve(work_r), carve(work_f)
        qk_hi, qk_lo = tr(4, S), tr(4, S)
        v_hi, v_lo = tr(QT, H), tr(QT, H)
        p_hi, p_lo = tr(QT, S), tr(QT, S)
        c_hi, c_lo = qk_hi[:, 0:2, :], qk_lo[:, 0:2, :]
        vt = tf(KH, S)
        prob = tf(QT, S)
        sm = tf(4, QT)

        tr, tf = carve(work_r), carve(work_f)
        qc_hi, qc_lo = tr(KH, S), tr(KH, S)
        kc_hi, kc_lo = tr(S), tr(S)
        qs = [tr(S) for _ in range(2)]
        qm = [tr(S) for _ in range(2)]
        ks = [tr(S) for _ in range(3)]
        on_hi, on_lo = tr(KH, S), tr(KH, S)
        mz = tr(QT, R, 32)
        kv = tf(S)
        va = tf(QT, NG, 32)
        pt = [tf(R, S) for _ in range(2)]
        ot = tf(S)
        on = tf(QT, H)
        mx = tf(2, QT * R)
        rec = tf(QT * R)

        tr, tf = carve(work_r), carve(work_f)
        fw_hi, fw_lo = tr(NF0, WS), tr(NF0, WT)
        h_hi, h_lo = tr(4, S), tr(4, S)
        sg, su, hh = tf(2, S), tf(2, S), tf(2, S)
        tf = carve(work_f)
        cmp_a, cmp_b = tf(8, E0, E0), tf(8, E0, E0)

        s_x, s_c = [sem(f"s_xin{b}") for b in range(B)], sem("s_c")
        s_raw, s_split, s_wh = sem("s_raw"), sem("s_split"), sem("s_wh")
        s_dve, s_sq, s_ve = sem("s_dve"), sem("s_sq"), sem("s_ve")
        s_xn, s_xnT, s_xh, s_xl = sem("s_xn"), sem("s_xnT"), sem("s_xh"), sem("s_xl")
        s_lg, s_ex, s_exd = sem("s_lg"), sem("s_ex"), sem("s_exd")
        s_gw, s_gt, s_wt = sem("s_gw"), sem("s_gt"), sem("s_wt")
        s_ws = sem("s_ws")
        a_pj, a_hi, a_lo, a_vt, a_vx = sem("a_pj"), sem("a_hi"), sem("a_lo"), sem("a_vt"), sem("a_vx")
        a_vh, a_vl, a_sc, a_m, a_n = sem("a_vh"), sem("a_vl"), sem("a_sc"), sem("a_m"), sem("a_n")
        a_e, a_r, a_p, a_pt, a_ph, a_pl = (sem(n) for n in ("a_e", "a_r", "a_p", "a_pt", "a_ph", "a_pl"))
        a_cx, a_ch, a_cl, a_o, a_y = (sem(n) for n in ("a_cx", "a_ch", "a_cl", "a_o", "a_y"))
        f_gu, f_s, f_p, f_h, f_hi, f_lo, f_dn, f_y = (
            [sem(f"{n}{i}") for i in range(2)] for n in ("f_gu", "f_s", "f_p", "f_h", "f_hi", "f_lo", "f_dn", "f_y"))
        s_yt, s_x1, s_out = sem("s_yt"), sem("s_x1"), sem("s_out")
        b_pj, b_kv, b_hi, b_lo, b_vt, b_va = (sem(n) for n in ("b_pj", "b_kv", "b_hi", "b_lo", "b_vt", "b_va"))
        b_sq, b_qs, b_sk, b_ks, b_sn, b_mx = (sem(n) for n in ("b_sq", "b_qs", "b_sk", "b_ks", "b_sn", "b_mx"))
        b_m1, b_m2, b_mt, b_qm, b_st, b_ex = (sem(n) for n in ("b_m1", "b_m2", "b_mt", "b_qm", "b_st", "b_ex"))
        b_pv, b_ot, b_ox, b_rc, b_on, b_nt = (sem(n) for n in ("b_pv", "b_ot", "b_ox", "b_rc", "b_on", "b_nt"))
        b_nh, b_nl, b_o, b_y = (sem(n) for n in ("b_nh", "b_nl", "b_o", "b_y"))

        block = ctx.enter_context(nc.Block())

        SPLIT_A0 = 1
        SPLIT_F0 = SPLIT_A0
        SPLIT_A1 = SPLIT_F0 + G0 * NF0 + 1
        SPLIT_F1 = SPLIT_A1

        @block.sync
        def _(sp):
            for b in range(B):
                sp.dma_start(x[:, b * QT:(b + 1) * QT, :],
                             x_in[b * S:(b + 1) * S, :].rearrange("(t p) h -> p t h", p=P)).then_inc(s_x[b], 16)
            sp.dma_start(const[:], const_in).then_inc(s_c, 16)
            sp.dma_start(bias[:], bias_in).then_inc(s_c, 16)
            sp.dma_start(raw[:, 0:AW0], aw0_in).then_inc(s_raw, 16)
            with sp.Fori(0, G0) as g:
                sp.wait_ge(s_split, g * NF0 + SPLIT_F0)
                sp.dma_start(raw[:], ffn0_in[bass.ts(g, P), :]).then_inc(s_raw, 16)
            sp.wait_ge(s_split, SPLIT_F0 + G0 * NF0)
            sp.dma_start(raw[:, 0:AW1], aw1_in).then_inc(s_raw, 16)
            sp.dma_start(raw[:, AW1:AW1 + NSELQ + NSELK], sel_in).then_inc(s_raw, 16)
            with sp.Fori(0, G1) as g:
                sp.wait_ge(s_split, g * NF1 + SPLIT_F1)
                sp.dma_start(raw[:, 0:NF1 * WS], ffn1_in[bass.ts(g, P), :]).then_inc(s_raw, 16)
            for i in range(TT // 2):
                sp.wait_ge(s_x1, TT // 2 + i + 1)
                sp.dma_start(out[2 * i * P:(2 * i + 2) * P, :].rearrange("(t p) h -> p t h", p=P),
                             x[:, 2 * i:2 * i + 2, :]).then_inc(s_out, 16)
            sp.wait_ge(s_out, 16 * (TT // 2))

        @block.gpsimd
        def _(pool):
            pool.wait_ge(s_raw, 16)
            nc.gpsimd.tensor_copy(awr[:, 0:AW0], raw[:, 0:AW0]).then_inc(s_wh, 1)
            pool.wait_ge(s_wh, 1)
            nc.gpsimd.tensor_tensor(awr[:, AW0:2 * AW0], raw[:, 0:AW0], awr[:, 0:AW0].bitcast(f32),
                                    ALU.subtract).then_inc(s_split, 1)
            nh = 1

            def split_tile(f, nf, wh):
                hi = nc.gpsimd.tensor_copy(fw_hi[:, f, :], raw[:, f * WS:(f + 1) * WS])
                hi.then_inc(s_wh, 1)
                pool.wait_ge(s_wh, wh)
                nc.gpsimd.tensor_tensor(fw_lo[:, f, :], raw[:, f * WS:f * WS + WT],
                                        fw_hi[:, f, 0:WT].bitcast(f32), ALU.subtract).then_inc(s_split, 1)

            pool.wait_ge(s_raw, 2 * 16)
            pool.wait_ge(a_y, 2 * B)
            for f in range(NF0):
                split_tile(f, NF0, 1 + f + 1)
            for g in range(1, G0):
                pool.wait_ge(s_raw, g * 16 + 2 * 16)
                for f in range(NF0):
                    pool.wait_ge(f_dn[0], g * (B * NF0) + (f + 1 - NF0))
                    split_tile(f, NF0, g * NF0 + (1 + f + 1))
            pool.wait_ge(s_raw, (G0 + 3) * 16)
            nc.gpsimd.tensor_copy(awr[:, 0:AW1], raw[:, 0:AW1]).then_inc(s_wh, 1)
            pool.wait_ge(s_wh, 1 + G0 * NF0 + 1)
            nc.gpsimd.tensor_copy(awr[:, 2 * AW1:2 * AW1 + NSELQ + NSELK], raw[:, AW1:AW1 + NSELQ + NSELK])
            nc.gpsimd.tensor_tensor(awr[:, AW1:2 * AW1], raw[:, 0:AW1], awr[:, 0:AW1].bitcast(f32),
                                    ALU.subtract).then_inc(s_split, 1)
            pool.wait_ge(s_raw, (G0 + 4) * 16)
            pool.wait_ge(b_y, 2 * B)
            for f in range(NF1):
                split_tile(f, NF1, 2 + G0 * NF0 + f + 1)
            for g in range(1, G1):
                pool.wait_ge(s_raw, g * 16 + (G0 + 4) * 16)
                for f in range(NF1):
                    pool.wait_ge(f_dn[1], g * (B * NF1) + (f + 1 - NF1))
                    split_tile(f, NF1, g * NF1 + (2 + G0 * NF0 + f + 1))

        @block.tensor
        def _(pe):
            def mm3(o, w_hi, w_lo, x_hi, x_lo, first, last):
                nc.tensor.matmul(o, w_hi, x_hi, start=first, stop=False)
                nc.tensor.matmul(o, w_hi, x_lo, start=False, stop=False)
                return nc.tensor.matmul(o, w_lo, x_hi, start=False, stop=last)

            def norm_and_gate(layer, whi, wlo, ne):
                for b in range(B):
                    for k in range(KH):
                        for t in range(QT):
                            if k == 0:
                                pe.wait_ge(s_xn, layer * TT + b * QT + t + 1)
                            ins = nc.tensor.transpose(psum[:, 2 * b + k, t * P:(t + 1) * P],
                                                      xn[:, b * QT + t, k * P:(k + 1) * P], ident)
                        ins.then_inc(s_xnT, 1)
                pe.wait_ge(s_xl, (layer + 1) * 2 * B)
                pe.wait_ge(s_split, SPLIT_A1 if layer else SPLIT_A0)
                for t in range(TT):
                    o = psum[:, 0, t * ne:(t + 1) * ne]
                    for k in range(KH):
                        ins = mm3(o, xt_hi[:, k, t * P:(t + 1) * P], xt_lo[:, k, t * P:(t + 1) * P],
                                  whi[2][:, k, :], wlo[2][:, k, :], k == 0, k == KH - 1)
                ins.then_inc(s_lg, 1)

            def gating_transposes(layer, cols):
                pe.wait_ge(s_gw, layer + 1)
                for t in range(TT):
                    ins = nc.tensor.transpose(psum[:, 4 + t // 4, (t % 4) * P:(t % 4 + 1) * P],
                                              gw[:, t * cols:t * cols + P].bitcast(f32), ident)
                ins.then_inc(s_gt, 1)
                pe.wait_ge(s_wt, layer + 1)

            def feed_forward(layer, nf, groups, split0):
                gu, h, lo, dn, yf = (s[layer] for s in (f_gu, f_h, f_lo, f_dn, f_y))
                nt = B * nf
                rows = LN_COLS1 if layer else LN_COLS

                def up(j, g, g_off):
                    k, f = j // nf, j % nf
                    pe.wait_ge(s_split, g * nf + (split0 + f + 1 + g_off * nf))
                    if not (isinstance(g, int) and j < 2):
                        pe.wait_ge(h, g * nt + (j - 1 + g_off * nt))
                    tok = slice(k * S, (k + 1) * S)
                    for c in range(2):
                        for i in range(KH):
                            col = (c * KH + i) * P
                            mm3(psum[:, 2 * c + j % 2, :], fw_hi[:, f, col:col + P], fw_lo[:, f, col:col + P],
                                xt_hi[:, i, tok], xt_lo[:, i, tok], i == 0, i == KH - 1)
                    nc.tensor.matmul(psum[:, 4 + j % 2, :], fw_hi[0:rows, f, WT:WS], wt[0:rows, tok],
                                     start=True, stop=True).then_inc(gu, 1)

                def down(j, g):
                    k, f = j // nf, j % nf
                    pe.wait_ge(lo, g * nt + (j + 1))
                    if f == 0:
                        pe.wait_ge(yf, g * B + (k + 1))
                    for c in range(KH):
                        col = WC + c * P
                        ins = mm3(psum[:, 6 + c, :], fw_hi[:, f, col:col + P], fw_lo[:, f, col:col + P],
                                  h_hi[:, j % 4, :], h_lo[:, j % 4, :], f == 0, f == nf - 1)
                    ins.then_inc(dn, 1)

                up(0, 0, 0)
                up(1, 0, 0)
                with pe.Fori(0, groups - 1) as g:
                    for j in range(nt):
                        if j + 2 < nt:
                            up(j + 2, g, 0)
                        else:
                            up(j + 2 - nt, g, 1)
                        down(j, g)
                for j in range(nt):
                    if j + 2 < nt:
                        up(j + 2, groups - 1, 0)
                    down(j, groups - 1)

            def sum_to_tokens(layer):
                pe.wait_ge(f_y[layer], (G1 if layer else G0) * B + 1)
                for t in range(TT):
                    for k in range(KH):
                        ins = nc.tensor.transpose(psum[:, t // 2, (t % 2) * H + k * P:(t % 2) * H + (k + 1) * P],
                                                  yacc[:, k, t * P:(t + 1) * P], ident)
                    if t % 2:
                        ins.then_inc(s_yt, 1)

            pe.wait_ge(s_c, 32)
            norm_and_gate(0, w0_hi, w0_lo, E0)
            gating_transposes(0, LN_COLS)
            with pe.Fori(0, B) as b:
                for n in range(6):
                    for i in range(KH):
                        ins = mm3(psum[:, n, :], w0_hi[0][:, i, n * P:(n + 1) * P], w0_lo[0][:, i, n * P:(n + 1) * P],
                                  xt_hi[:, i, bass.ts(b, S)], xt_lo[:, i, bass.ts(b, S)], i == 0, i == KH - 1)
                    ins.then_inc(a_pj, 1)
                pe.wait_ge(a_vt, b * 2 + 2)
                for t in range(QT):
                    for c in range(KH):
                        ins = nc.tensor.transpose(psum[:, 6 + t // 2, (t % 2) * H + c * P:(t % 2) * H + (c + 1) * P],
                                                  vt[:, c, t * P:(t + 1) * P], ident)
                    if t % 2:
                        ins.then_inc(a_vx, 1)
                pe.wait_ge(a_lo, b * 4 + 4)
                for t in range(QT):
                    for i in range(KH):
                        q = slice(t * P, (t + 1) * P)
                        ins = mm3(psum[:, t, :], qk_hi[:, i, q], qk_lo[:, i, q], qk_hi[:, 2 + i, :],
                                  qk_lo[:, 2 + i, :], i == 0, i == KH - 1)
                    ins.then_inc(a_sc, 1)
                pe.wait_ge(a_vl, b * 2 + 2)
                for t in range(QT):
                    pe.wait_ge(a_p, b * QT + (t + 1))
                    for c in range(QT):
                        ins = nc.tensor.transpose(psum[:, 4 + t, c * P:(c + 1) * P], prob[:, t, c * P:(c + 1) * P], ident)
                    ins.then_inc(a_pt, 1)
                pe.wait_ge(a_pl, b * QT + QT)
                for c in range(KH):
                    for t in range(QT):
                        ins = mm3(psum[:, c, :], v_hi[:, t, c * P:(c + 1) * P], v_lo[:, t, c * P:(c + 1) * P],
                                  p_hi[:, t, :], p_lo[:, t, :], t == 0, t == QT - 1)
                    ins.then_inc(a_cx, 1)
                pe.wait_ge(a_cl, b * 2 + 2)
                for c in range(KH):
                    for i in range(KH):
                        ins = mm3(psum[:, 2 + c, :], w0_hi[1][:, i, c * P:(c + 1) * P], w0_lo[1][:, i, c * P:(c + 1) * P],
                                  c_hi[:, i, :], c_lo[:, i, :], i == 0, i == KH - 1)
                    ins.then_inc(a_o, 1)
                pe.wait_ge(a_y, b * 2 + 2)
            feed_forward(0, NF0, G0, SPLIT_F0)
            sum_to_tokens(0)
            norm_and_gate(1, w1_hi, w1_lo, E1 + 1)
            gating_transposes(1, LN_COLS1)
            NP = NG * QT * R
            with pe.Fori(0, B) as b:
                for n in range(3):
                    for i in range(KH):
                        ins = mm3(psum[:, 1 + n, :], w1_hi[0][:, i, n * P:(n + 1) * P], w1_lo[0][:, i, n * P:(n + 1) * P],
                                  xt_hi[:, i, bass.ts(b, S)], xt_lo[:, i, bass.ts(b, S)], i == 0, i == KH - 1)
                    ins.then_inc(b_pj, 1)
                pe.wait_ge(b_kv, b + 1)
                for t in range(QT):
                    ins = nc.tensor.transpose(psum[:, 4, t * P:(t + 1) * P], kv[:, t * P:(t + 1) * P], ident)
                ins.then_inc(b_vt, 1)
                pe.wait_ge(b_lo, b * 3 + 3)
                pe.wait_ge(b_va, b + 1)

                def stack_q(g):
                    if g >= 2:
                        pe.wait_ge(b_qm, b * NG + (g - 1))
                    nc.tensor.matmul(psum[:, 0, :], selq[:, 0, g % 4, :], qc_hi[:, g // 4, :], start=True, stop=False)
                    nc.tensor.matmul(psum[:, 0, :], selq[:, 1, g % 4, :], qc_lo[:, g // 4, :],
                                     start=False, stop=True).then_inc(b_sq, 1)

                def stack_k(g):
                    pe.wait_ge(b_qs, b * NG + (g + 1))
                    nc.tensor.matmul(psum[:, 0, :], selk[0:64, 0, g, :], kc_hi[0:64, :], start=True, stop=False)
                    nc.tensor.matmul(psum[:, 0, :], selk[0:64, 1, g, :], kc_lo[0:64, :],
                                     start=False, stop=True).then_inc(b_sk, 1)

                def scores(g, t, r):
                    n = (g * QT + t) * R + r
                    if n >= 2:
                        pe.wait_ge(b_mx, b * NP + (n - 1))
                    q = 32 * r
                    nc.tensor.matmul(psum[:, 1 + n % 2, :], qs[g % 2][q:q + 26, t * P:(t + 1) * P],
                                     ks[g % 3][q:q + 26, :], start=True, stop=True,
                                     tile_position=(q, 0)).then_inc(b_sn, 1)

                def scores_t(g, t, h):
                    n = (g * QT + t) * 2 + h
                    if n >= 2:
                        pe.wait_ge(b_ex, b * (NP // 2) + (n - 1))
                    for r in (2 * h, 2 * h + 1):
                        ins = nc.tensor.matmul(psum[:, 3 + 2 * h + r % 2, :], ks[g % 3][32 * r:32 * r + 26, t * P:(t + 1) * P],
                                               qm[g % 2][32 * r:32 * r + 26, :], start=True, stop=True,
                                               tile_position=(32 * r, 0))
                    ins.then_inc(b_st, 1)

                def values(g, t):
                    pe.wait_ge(b_ex, b * (NP // 2) + ((g * QT + t) * 2 + 2))
                    if t == 0 and g >= 1:
                        pe.wait_ge(b_ot, b * NG + g)
                    for r in range(R):
                        ins = nc.tensor.matmul(psum[32 * r:32 * r + 32, 7, :], va[:, t, g, :], pt[t % 2][:, r, :],
                                               start=(t == 0), stop=(t == QT - 1), tile_position=(0, 32 * r))
                    ins.then_inc(b_pv, 1)

                def outputs_t(g):
                    pe.wait_ge(b_ot, b * NG + (g + 1))
                    for t in range(QT):
                        ins = nc.tensor.transpose(psum[:, 0, t * P:(t + 1) * P], ot[:, t * P:(t + 1) * P], ident)
                    ins.then_inc(b_ox, 1)

                def maxima_t(g):
                    pe.wait_ge(b_m2, b * NG + (g + 1))
                    for t in range(QT):
                        ins = nc.tensor.transpose(psum[:, 0, t * P:(t + 1) * P],
                                                  mz[:, t].rearrange("p r c -> p (r c)").bitcast(f32), ident)
                    ins.then_inc(b_mt, 1)

                stack_q(0)
                stack_k(0)
                pe.wait_ge(b_ks, b * NG + 1)
                for s in range(NG + 1):
                    front, back = s < NG, s >= 1
                    if front and s >= 1:
                        pe.wait_ge(b_ks, b * NG + (s + 1))
                    if back:
                        pe.wait_ge(b_qm, b * NG + s)
                    for t in range(QT):
                        if front:
                            scores(s, t, 0)
                        if back:
                            scores_t(s - 1, t, 0)
                        if front:
                            scores(s, t, 1)
                        if back:
                            scores_t(s - 1, t, 1)
                        if front:
                            scores(s, t, 2)
                        if back and t >= 1:
                            values(s - 1, t - 1)
                        if front:
                            scores(s, t, 3)
                        if t == 0 and s + 1 < NG:
                            stack_q(s + 1)
                        if t == 1 and s + 1 < NG:
                            stack_k(s + 1)
                        if t == 2 and s >= 2:
                            if s + 1 < NG:
                                pe.wait_ge(b_ks, b * NG + (s + 2))
                            elif s < NG:
                                pe.wait_ge(b_qm, b * NG + s)
                            outputs_t(s - 2)
                    if back:
                        values(s - 1, QT - 1)
                    if front:
                        if s >= 2:
                            pe.wait_ge(b_on, b * NG + (s - 1))
                        elif s + 1 < NG:
                            pe.wait_ge(b_ks, b * NG + (s + 2))
                        maxima_t(s)
                pe.wait_ge(b_on, b * NG + (NG - 1))
                outputs_t(NG - 1)
                pe.wait_ge(b_on, b * NG + NG)
                for c in range(KH):
                    for t in range(QT):
                        ins = nc.tensor.transpose(psum[:, 1 + c, t * P:(t + 1) * P], on[:, t, c * P:(c + 1) * P], ident)
                    ins.then_inc(b_nt, 1)
                pe.wait_ge(b_nl, b * 2 + 2)
                for c in range(KH):
                    for i in range(KH):
                        ins = mm3(psum[:, 3 + c, :], w1_hi[1][:, i, c * P:(c + 1) * P], w1_lo[1][:, i, c * P:(c + 1) * P],
                                  on_hi[:, i, :], on_lo[:, i, :], i == 0, i == KH - 1)
                    ins.then_inc(b_o, 1)
                pe.wait_ge(b_y, b * 2 + 2)
            feed_forward(1, NF1, G1, SPLIT_F1)
            sum_to_tokens(1)

        @block.scalar
        def _(act):
            def copy(o, i):
                return nc.scalar.copy(o, i)

            def norm_and_gate(layer, ne):
                act.wait_ge(s_ve, layer + 1)
                nc.scalar.activation(rs[:, 1, :], rs[:, 0, :], ACT.Sqrt).then_inc(s_sq, 1)
                for n in range(2 * B):
                    act.wait_ge(s_xnT, layer * 2 * B + n + 1)
                    b, k = n // KH, n % KH
                    copy(xt_hi[:, k, b * S:(b + 1) * S], psum[:, n, :]).then_inc(s_xh, 1)
                act.wait_ge(s_ex, layer + 1)
                nc.scalar.activation(pr[:, :, 0:ne], pr[:, :, 0:ne], ACT.Exp).then_inc(s_exd, 1)
                act.wait_ge(s_gt, layer + 1)
                rows = LN_COLS1 if layer else LN_COLS
                copy(wt[0:rows, :].rearrange("p (a b) -> p a b", a=B), psum[0:rows, 4:8, :]).then_inc(s_wt, 1)

            def feed_forward(layer, nf, groups):
                gu, s, h, hi = (q[layer] for q in (f_gu, f_s, f_h, f_hi))
                nt = B * nf
                with act.Fori(0, groups) as g:
                    for j in range(nt):
                        act.wait_ge(gu, g * nt + (j + 1))
                        nc.scalar.activation(sg[:, j % 2, :], psum[:, j % 2, :], ACT.Silu).then_inc(s, 1)
                        act.wait_ge(h, g * nt + (j + 1))
                        copy(h_hi[:, j % 4, :], hh[:, j % 2, :]).then_inc(hi, 1)

            norm_and_gate(0, E0)
            with act.Fori(0, B) as b:
                for n in range(4):
                    act.wait_ge(a_pj, b * 6 + (n + 1))
                    nc.scalar.activation(qk_hi[:, n, :], psum[:, n, :], ACT.Identity, bias=bq0[:, n:n + 1]).then_inc(a_hi, 1)
                for n in (4, 5):
                    act.wait_ge(a_pj, b * 6 + (n + 1))
                    nc.scalar.activation(vt[:, n - 4, :], psum[:, n, :], ACT.Identity, bias=bq0[:, n:n + 1]).then_inc(a_vt, 1)
                for c in range(2):
                    act.wait_ge(a_vx, b * 2 + (c + 1))
                    copy(v_hi[:, 2 * c:2 * c + 2, :], psum[:, 6 + c, :].rearrange("p (t h) -> p t h", h=H)).then_inc(a_vh, 1)
                for t in range(QT):
                    act.wait_ge(a_n, b * QT + (t + 1))
                    nc.scalar.activation(prob[:, t, :], psum[:, t, :], ACT.Exp, scale=1.0 / 16.0, bias=sm[:, 1, t:t + 1],
                                         accum_out=sm[:, 2, t:t + 1]).then_inc(a_e, 1)
                for t in range(QT):
                    act.wait_ge(a_pt, b * QT + (t + 1))
                    copy(p_hi[:, :, t * P:(t + 1) * P], psum[:, 4 + t, :].rearrange("p (c q) -> p c q", q=P)).then_inc(a_ph, 1)
                for c in range(KH):
                    act.wait_ge(a_cx, b * 2 + (c + 1))
                    copy(c_hi[:, c, :], psum[:, c, :]).then_inc(a_ch, 1)
                for c in range(KH):
                    act.wait_ge(a_o, b * 2 + (c + 1))
                    nc.scalar.activation(yacc[:, c, bass.ts(b, S)], psum[:, 2 + c, :], ACT.Identity,
                                         bias=bo0[:, c:c + 1]).then_inc(a_y, 1)
            feed_forward(0, NF0, G0)
            norm_and_gate(1, E1)
            with act.Fori(0, B) as b:
                for n in range(2):
                    act.wait_ge(b_pj, b * 3 + (n + 1))
                    nc.scalar.activation(qc_hi[:, n, :], psum[:, 1 + n, :], ACT.Identity, bias=bq1[:, n:n + 1]).then_inc(b_hi, 1)
                act.wait_ge(b_pj, b * 3 + 3)
                nc.scalar.activation(kv[:], psum[:, 3, :], ACT.Identity, bias=bq1[:, 2:3]).then_inc(b_kv, 1)
                nc.scalar.activation(kc_hi[:], psum[:, 3, :], ACT.Identity, bias=bq1[:, 2:3]).then_inc(b_hi, 1)

                def stacks(g, part):
                    if part == 0:
                        act.wait_ge(b_sq, b * NG + (g + 1))
                        copy(qs[g % 2], psum[:, 0, :]).then_inc(b_qs, 1)
                    else:
                        act.wait_ge(b_sk, b * NG + (g + 1))
                        nc.scalar.activation(ks[g % 3], psum[:, 0, :], ACT.Identity, bias=kone).then_inc(b_ks, 1)

                stacks(0, 0)
                stacks(0, 1)
                for s in range(NG + 1):
                    for t in range(QT):
                        if s >= 1:
                            g = s - 1
                            for h in range(2):
                                n = (g * QT + t) * 2 + h
                                act.wait_ge(b_st, b * (NG * QT * 2) + (n + 1))
                                if g * QT + t >= 2:
                                    act.wait_ge(b_pv, b * (NG * QT) + (g * QT + t - 1))
                                nc.scalar.activation(pt[t % 2][:, 2 * h:2 * h + 2, :], psum[:, 3 + 2 * h:5 + 2 * h, :],
                                                     ACT.Exp, scale=float(HD) ** -0.5).then_inc(b_ex, 1)
                        if t < 2 and s + 1 < NG:
                            stacks(s + 1, t)
                    if s >= 1:
                        act.wait_ge(b_pv, b * (NG * QT) + s * QT)
                        if s >= 2:
                            act.wait_ge(b_ox, b * NG + (s - 1))
                        copy(ot[:], psum[:, 7, :]).then_inc(b_ot, 1)
                for c in range(KH):
                    act.wait_ge(b_nt, b * 2 + (c + 1))
                    copy(on_hi[:, c, :], psum[:, 1 + c, :]).then_inc(b_nh, 1)
                for c in range(KH):
                    act.wait_ge(b_o, b * 2 + (c + 1))
                    nc.scalar.activation(yacc[:, c, bass.ts(b, S)], psum[:, 3 + c, :], ACT.Identity,
                                         bias=bo1[:, c:c + 1]).then_inc(b_y, 1)
            feed_forward(1, NF1, G1)

        @block.vector
        def _(dve):
            v = nc.vector
            done = [0]

            def then(ins):
                done[0] += 1
                ins.then_inc(s_dve, 1)
                dve.wait_ge(s_dve, done[0])

            def norm_and_gate(layer, ne, top):
                ne1 = ne + 1
                for t in range(TT):
                    if layer == 0 and t % QT == 0:
                        dve.wait_ge(s_x[t // QT], 16)
                    ins = v.bn_stats(st[:, t, :], x[:, t, :])
                then(ins)
                for t in range(TT):
                    ins = v.bn_aggr(mv[:, t, :], st[:, t, :])
                then(ins)
                ve, sd, r0, t1, rstd = (rs[:, i, :] for i in range(5))
                v.tensor_scalar_add(ve, mv[:, :, 1], EPS).then_inc(s_ve, 1)
                dve.wait_ge(s_sq, layer + 1)
                then(v.reciprocal(r0, sd))
                then(v.tensor_tensor(t1, r0, r0, ALU.mult))
                then(v.tensor_tensor(t1, t1, ve, ALU.mult))
                then(v.tensor_scalar(t1, t1, -0.5, 1.5, ALU.mult, ALU.add))
                then(v.tensor_tensor(rstd, r0, t1, ALU.mult))
                for t in range(TT):
                    v.tensor_scalar(xn[:, t, :], x[:, t, :], mv[:, t, 0:1], rs[:, 4, t:t + 1],
                                    ALU.subtract, ALU.mult).then_inc(s_xn, 1)
                for n in range(2 * B):
                    dve.wait_ge(s_xh, layer * 2 * B + n + 1)
                    b, k = n // KH, n % KH
                    tok = slice(b * S, (b + 1) * S)
                    v.tensor_tensor(xt_lo[:, k, tok], psum[:, n, :], xt_hi[:, k, tok].bitcast(f32),
                                    ALU.subtract).then_inc(s_xl, 1)
                dve.wait_ge(s_lg, layer + 1)
                cols = E0 if layer == 0 else E1 + 1
                raw_lg = psum[:, 0, 0:TT * cols].rearrange("p (t e) -> p t e", e=cols)[:, :, 0:ne]
                l, p, rk = lg[:, :, 0:ne], pr[:, :, 0:ne], rank[:, :, 0:ne]
                if layer == 0:
                    then(v.tensor_copy(l, raw_lg))
                else:
                    then(v.tensor_tensor(l, raw_lg, gate_b.unsqueeze(1).broadcast_to([P, TT, ne]), ALU.add))
                col = lambda i: rs[:, i, :].unsqueeze(2).broadcast_to([P, TT, ne])
                then(v.reduce_max(rs[:, 5, :], l, AX.X))
                v.tensor_tensor(p, l, col(5), ALU.subtract).then_inc(s_ex, 1)
                dve.wait_ge(s_exd, layer + 1)
                then(v.reduce_sum(rs[:, 6, :], p, AX.X))
                then(v.reciprocal(rs[:, 7, :], rs[:, 6, :]))
                then(v.tensor_tensor(p, p, col(7), ALU.mult))
                if layer == 1:
                    then(v.tensor_tensor(l, p, route_b.unsqueeze(1).broadcast_to([P, TT, ne]), ALU.add))
                low = (low0 if layer == 0 else low1).rearrange("p (a b) -> p a b", b=ne)
                for c in range(TT // 8):
                    lc = l[:, 8 * c:8 * c + 8, :]
                    other = lc.unsqueeze(2).broadcast_to([P, 8, ne, ne])
                    own = lc.unsqueeze(3).broadcast_to([P, 8, ne, ne])
                    ca, cb = cmp_a[:, :, 0:ne, 0:ne], cmp_b[:, :, 0:ne, 0:ne]
                    v.tensor_tensor(ca, other, own, ALU.is_gt)
                    then(v.tensor_tensor(cb, other, own, ALU.is_equal))
                    then(v.tensor_tensor(cb, cb, low.unsqueeze(1).broadcast_to([P, 8, ne, ne]), ALU.mult))
                    then(v.tensor_tensor(ca, ca, cb, ALU.add))
                    then(v.tensor_reduce(rk[:, 8 * c:8 * c + 8, :], ca, AX.X, ALU.add))
                then(v.tensor_scalar(rk, rk, float(top), None, ALU.is_lt))
                then(v.tensor_tensor(p, p, rk, ALU.mult))
                if layer == 1:
                    then(v.reduce_sum(rs[:, 6, :], p, AX.X))
                    then(v.reciprocal(rs[:, 7, :], rs[:, 6, :]))
                    then(v.tensor_tensor(p, p, col(7), ALU.mult))
                g = gw[:, 0:TT * 2 * ne1].rearrange("p (t c) -> p t c", c=2 * ne1)
                then(v.memset(gw[:].bitcast(mybir.dt.uint32), 0))
                v.memset(g[:, :, ne:ne1].bitcast(f32), 1.0)
                then(v.tensor_copy(g[:, :, 0:ne], p))
                v.tensor_tensor(g[:, :, ne1:ne1 + ne], p, g[:, :, 0:ne].bitcast(f32), ALU.subtract).then_inc(s_gw, 1)

            def feed_forward(layer, nf, groups):
                gu, s, sp_, h, hi, lo, dn, yf = (q[layer] for q in (f_gu, f_s, f_p, f_h, f_hi, f_lo, f_dn, f_y))
                nt = B * nf
                v.memset(rs[:, 7, 0:1], 0.0).then_inc(yf, 1)
                with dve.Fori(0, groups) as g:
                    def add_outputs(k):
                        dve.wait_ge(dn, g * nt + (k + 1) * nf)
                        tok = slice(k * S, (k + 1) * S)
                        v.tensor_tensor(yacc[:, :, tok], yacc[:, :, tok], psum[:, 6:8, :], ALU.add).then_inc(yf, 1)

                    for j in range(nt):
                        dve.wait_ge(s, g * nt + (j + 1))
                        v.tensor_tensor(su[:, j % 2, :], sg[:, j % 2, :], psum[:, 2 + j % 2, :], ALU.mult).then_inc(sp_, 1)
                        dve.wait_ge(sp_, g * nt + (j + 1))
                        v.tensor_tensor(hh[:, j % 2, :], su[:, j % 2, :], psum[:, 4 + j % 2, :], ALU.mult).then_inc(h, 1)
                        dve.wait_ge(hi, g * nt + (j + 1))
                        v.tensor_tensor(h_lo[:, j % 4, :], hh[:, j % 2, :], h_hi[:, j % 4, :].bitcast(f32),
                                        ALU.subtract).then_inc(lo, 1)
                        if j % nf == 1 and j > nf:
                            add_outputs(j // nf - 1)
                    add_outputs(B - 1)

            def residual(layer):
                for i in range(TT // 2):
                    dve.wait_ge(s_yt, layer * (TT // 2) + i + 1)
                    v.tensor_tensor(x[:, 2 * i:2 * i + 2, :], x[:, 2 * i:2 * i + 2, :],
                                    psum[:, i, :].rearrange("p (t h) -> p t h", h=H), ALU.add).then_inc(s_x1, 1)

            dve.wait_ge(s_c, 32)
            norm_and_gate(0, E0, TOP0)
            with dve.Fori(0, B) as b:
                for n in range(4):
                    dve.wait_ge(a_hi, b * 4 + (n + 1))
                    v.scalar_tensor_tensor(out=qk_lo[:, n, :], in0=psum[:, n, :], scalar=bq0[:, n:n + 1],
                                           in1=qk_hi[:, n, :].bitcast(f32), op0=ALU.add, op1=ALU.subtract).then_inc(a_lo, 1)
                for c in range(2):
                    dve.wait_ge(a_vh, b * 2 + (c + 1))
                    v.tensor_tensor(v_lo[:, 2 * c:2 * c + 2, :], psum[:, 6 + c, :].rearrange("p (t h) -> p t h", h=H),
                                    v_hi[:, 2 * c:2 * c + 2, :].bitcast(f32), ALU.subtract).then_inc(a_vl, 1)
                for t in range(QT):
                    dve.wait_ge(a_sc, b * QT + (t + 1))
                    v.reduce_max(sm[:, 0, t:t + 1], psum[:, t, :], AX.X).then_inc(a_m, 1)
                    dve.wait_ge(a_m, b * QT + (t + 1))
                    v.tensor_scalar(sm[:, 1, t:t + 1], sm[:, 0, t:t + 1], -1.0 / 16.0, None, ALU.mult).then_inc(a_n, 1)
                for t in range(QT):
                    dve.wait_ge(a_e, b * QT + (t + 1))
                    v.reciprocal(sm[:, 3, t:t + 1], sm[:, 2, t:t + 1]).then_inc(a_r, 1)
                    dve.wait_ge(a_r, b * QT + (t + 1))
                    v.tensor_scalar(prob[:, t, :], prob[:, t, :], sm[:, 3, t:t + 1], None, ALU.mult).then_inc(a_p, 1)
                for t in range(QT):
                    dve.wait_ge(a_ph, b * QT + (t + 1))
                    q = slice(t * P, (t + 1) * P)
                    v.tensor_tensor(p_lo[:, :, q], psum[:, 4 + t, :].rearrange("p (c q) -> p c q", q=P),
                                    p_hi[:, :, q].bitcast(f32), ALU.subtract).then_inc(a_pl, 1)
                for c in range(KH):
                    dve.wait_ge(a_ch, b * 2 + (c + 1))
                    v.tensor_tensor(c_lo[:, c, :], psum[:, c, :], c_hi[:, c, :].bitcast(f32), ALU.subtract).then_inc(a_cl, 1)
            feed_forward(0, NF0, G0)
            residual(0)
            dve.wait_ge(s_x1, TT // 2)
            norm_and_gate(1, E1, TOP1)
            then(v.memset(va[:], 0.0))
            v.memset(va[:, :, :, HD:HD + 1], 1.0)
            then(v.memset(mz[:].bitcast(mybir.dt.uint32), 0))
            NP = NG * QT * R
            with dve.Fori(0, B) as b:
                for n in range(2):
                    dve.wait_ge(b_hi, b * 3 + (n + 1))
                    v.scalar_tensor_tensor(out=qc_lo[:, n, :], in0=psum[:, 1 + n, :], scalar=bq1[:, n:n + 1],
                                           in1=qc_hi[:, n, :].bitcast(f32), op0=ALU.add, op1=ALU.subtract).then_inc(b_lo, 1)
                dve.wait_ge(b_hi, b * 3 + 3)
                v.tensor_tensor(kc_lo[:], kv[:], kc_hi[:].bitcast(f32), ALU.subtract).then_inc(b_lo, 1)
                dve.wait_ge(b_vt, b + 1)
                v.tensor_copy(va[:, :, :, 0:HD], psum[:, 4, :].rearrange("p (t c) -> p t c", c=P)[:, :, 64:128]
                              .rearrange("p t (g d) -> p t g d", d=HD)).then_inc(b_va, 1)

                def normalise(g):
                    dve.wait_ge(b_ox, b * NG + (g + 1))
                    o = psum[:, 0, :].rearrange("p (q c) -> p q c", c=32)
                    v.reciprocal(rec[:].unsqueeze(2), o[:, :, HD:HD + 1]).then_inc(b_rc, 1)
                    dve.wait_ge(b_rc, b * NG + (g + 1))
                    v.tensor_tensor(on[:, :, g * 32:(g + 1) * 32].rearrange("p t (r d) -> p t r d", d=HD),
                                    o[:, :, 0:HD].rearrange("p (t r) d -> p t r d", r=R),
                                    rec[:].rearrange("p (t r) -> p t r", r=R).unsqueeze(3).broadcast_to([P, QT, R, HD]),
                                    ALU.mult).then_inc(b_on, 1)

                for s in range(NG + 1):
                    if s < NG:
                        for t in range(QT):
                            for r in range(R):
                                n = (s * QT + t) * R + r
                                dve.wait_ge(b_sn, b * NP + (n + 1))
                                v.reduce_max(mx[:, s % 2, t * R + r:t * R + r + 1], psum[:, 1 + n % 2, :], AX.X).then_inc(b_mx, 1)
                        dve.wait_ge(b_mx, b * NP + (s + 1) * QT * R)
                        if s >= 1:
                            dve.wait_ge(b_mt, b * NG + s)
                        m = mx[:, s % 2, :].unsqueeze(2)
                        z = mz[:].rearrange("p t r c -> p (t r) c")
                        v.tensor_scalar(z[:, :, 24:25], m, -1.0, None, ALU.mult).then_inc(b_m1, 1)
                        dve.wait_ge(b_m1, b * NG + (s + 1))
                        v.scalar_tensor_tensor(out=z[:, :, 25:26], in0=m, scalar=-1.0, in1=z[:, :, 24:25].bitcast(f32),
                                               op0=ALU.mult, op1=ALU.subtract).then_inc(b_m2, 1)
                    if s >= 2:
                        normalise(s - 2)
                    if s < NG:
                        dve.wait_ge(b_mt, b * NG + (s + 1))
                        v.tensor_tensor(qm[s % 2], psum[:, 0, :], qs[s % 2].bitcast(f32), ALU.add).then_inc(b_qm, 1)
                normalise(NG - 1)
                for c in range(KH):
                    dve.wait_ge(b_nh, b * 2 + (c + 1))
                    v.tensor_tensor(on_lo[:, c, :], psum[:, 1 + c, :], on_hi[:, c, :].bitcast(f32), ALU.subtract).then_inc(b_nl, 1)
            feed_forward(1, NF1, G1)
            residual(1)


def kernel(**inputs):
    import numpy as np
    import concourse.bacc as bacc
    from concourse.bass_utils import run_bass_kernel_spmd

    a = {k: np.ascontiguousarray(v) for k, v in inputs.items()}
    zeros = lambda *s: np.zeros(s, np.float32)

    def halves(w):
        return w.reshape(KH, P, -1).transpose(1, 0, 2).reshape(P, -1)

    def columns(vec):
        return vec.reshape(-1, P).T

    aw0 = np.concatenate([halves(a["L0_attn_w_qkv"].T), halves(a["L0_attn_w_out"].T),
                          halves(a["L0_ffn_gate_weight"].T)], 1)
    gate1 = np.concatenate([a["L1_ffn_gate_w"], zeros(H, 1)], 1)
    aw1 = np.concatenate([halves(a["L1_attn_w_qkv"].T), halves(a["L1_attn_w_out"].T), halves(gate1)], 1)

    def ffn(gate, up, down, groups, nf, hidden_expert, experts):
        tiles = groups * nf
        out = zeros(groups, P, nf, WS)
        for n in range(tiles):
            g, f = n // nf, n % nf
            c = slice(n * P, (n + 1) * P)
            out[g, :, f, 0:KH * P] = halves(gate[:, c])
            out[g, :, f, KH * P:WC] = halves(up[:, c])
            out[g, :, f, WC:WT] = down[c]
            for r in range(P):
                e = hidden_expert(n * P + r)
                out[g, e, f, WT + r] = 1.0
                out[g, experts + 1 + e, f, WT + r] = 1.0
        return out.reshape(groups * P, nf * WS)

    def wide(w):
        return w.transpose(1, 0, 2).reshape(H, -1)

    pad = G0 * NF0 * P - E0 * F0 - FS0
    ffn0 = ffn(np.concatenate([wide(a["L0_ffn_w_gate"]), a["L0_ffn_ws_gate"], zeros(H, pad)], 1),
               np.concatenate([wide(a["L0_ffn_w_up"]), a["L0_ffn_ws_up"], zeros(H, pad)], 1),
               np.concatenate([a["L0_ffn_w_down"].reshape(-1, H), a["L0_ffn_ws_down"], zeros(pad, H)], 0),
               G0, NF0, lambda i: min(i // F0, E0), E0)
    ffn1 = ffn(np.concatenate([wide(a["L1_ffn_W1"]), a["L1_ffn_Ws1"]], 1),
               np.concatenate([wide(a["L1_ffn_Wg"]), a["L1_ffn_Wsg"]], 1),
               np.concatenate([a["L1_ffn_W2"].reshape(-1, H), a["L1_ffn_Ws2"]], 0),
               G1, NF1, lambda i: i // F1, E1)

    selq, selk = zeros(P, 2, 4, P), zeros(P, 2, NG, P)
    for r in range(R):
        for d in range(HD):
            for slot, part in enumerate((0, 0, 1)):
                for j in range(4):
                    selq[j * 32 + r * HD + d, part, j, 32 * r + slot * HD + d] = 1.0
            for slot, part in enumerate((0, 1, 0)):
                for g in range(NG):
                    selk[g * HD + d, part, g, 32 * r + slot * HD + d] = 1.0
    sel = np.concatenate([selq.reshape(P, -1), selk.reshape(P, -1)], 1)
    const = zeros(P, CF)
    const[:, 0:P] = np.eye(P, dtype=np.float32)
    for r in range(R):
        const[32 * r + 3 * HD:32 * r + 3 * HD + 2, P] = 1.0
    for e in range(E0):
        const[:, P + 1 + e * E0:P + 1 + e * E0 + e] = 1.0
    for e in range(E1):
        const[:, P + 1 + E0 * E0 + e * E1:P + 1 + E0 * E0 + e * E1 + e] = 1.0
    bias = np.concatenate([columns(a["L0_attn_b_qkv"]), columns(a["L0_attn_b_out"]),
                           columns(a["L1_attn_b_qkv"]), columns(a["L1_attn_b_out"]),
                           np.broadcast_to(a["L1_ffn_gate_b"], (P, E1)),
                           np.broadcast_to(a["L1_ffn_biases"], (P, E1))], 1)

    host = {"x": a["L0_attn_hidden_states"].reshape(T, H), "aw0": aw0, "aw1": aw1, "sel": sel,
            "ffn0": ffn0, "ffn1": ffn1, "const": const, "bias": bias}
    nc = bacc.Bacc("TRN2", target_bir_lowering=False, num_devices=1)
    arrays, args = {}, []
    for name, value in host.items():
        arrays[f"in_{name}"] = np.ascontiguousarray(value)
        args.append(nc.dram_tensor(f"in_{name}", value.shape, mybir.dt.float32, kind="ExternalInput").ap())
    args.append(nc.dram_tensor("out_0", (T, H), mybir.dt.float32, kind="ExternalOutput").ap())
    program(nc, *args)
    r = run_bass_kernel_spmd(nc, [arrays], core_ids=[0])
    return r.results[0]["out_0"].reshape(B, S, H)
```

```python
import concourse.bass as bass
from concourse import mybir
from contextlib import ExitStack

P = 128
B, S, H = 4, 512, 256
T = B * S
TT = T // P
KH = H // P
QT = S // P
E0, TOP0, F0, FS0 = 16, 4, 176, 352
E1, TOP1, F1 = 7, 3, 256
NF0, G0 = 5, 5
NF1, G1 = 4, 4
WC = 2 * H + 2 * P + 0 + 0
WC = 2 * KH * P
WT = WC + H
WS = WT + P
NG, R, HD = 8, 4, 8
EPS = 1e-5
LN_COLS = 2 * (E0 + 1)
LN_COLS1 = 2 * (E1 + 1)
AW0 = KH * 3 * H + KH * H + KH * E0
AW1 = KH * (H + 2 * NG * HD) + KH * H + KH * (E1 + 1)
NSELQ = 2 * 4 * P
NSELK = 2 * NG * P
GATE_STEPS = 12
CF = P + 1 + E0 * E0 + E1 * E1 + R
BF = 6 + 2 + 3 + 2 + 2 * E1


def program(nc, x_in, aw0_in, aw1_in, sel_in, ffn0_in, ffn1_in, const_in, bias_in, out):
    f32, f32r = mybir.dt.float32, mybir.dt.float32r
    ALU, ACT, AX = mybir.AluOpType, mybir.ActivationFunctionType, mybir.AxisListType
    ctx = ExitStack()
    with ctx:
        def sb(name, shape, dt=f32):
            return ctx.enter_context(nc.sbuf_tensor(name, shape, dt))

        def sem(name):
            return ctx.enter_context(nc.semaphore(name))

        x = sb("x", [P, TT, H])
        yacc = sb("yacc", [P, KH, T])
        xn = yacc[:].rearrange("p k t -> p (k t)").rearrange("p (t h) -> p t h", h=H)
        xt_hi = sb("xt_hi", [P, KH, T], f32r)
        xt_lo = sb("xt_lo", [P, KH, T], f32r)
        wt = sb("wt", [P, T], f32r)
        raw = sb("raw", [P, NF0 * WS])
        awr = sb("awr", [P, max(2 * AW0, 2 * AW1 + NSELQ + NSELK)], f32r)
        const = sb("const", [P, CF])
        bias = sb("bias", [P, BF])
        st = sb("st", [P, TT, 6])
        mv = sb("mv", [P, TT, 2])
        zero = sb("zero", [P, 1])
        rs = sb("rs", [P, 8, TT])
        lg = sb("lg", [P, TT, E0])
        pr = sb("pr", [P, TT, E0])
        rank = sb("rank", [P, TT, E0])
        gw = sb("gw", [P, TT * LN_COLS + P], f32r)
        work_r = sb("work_r", [P, 13824], f32r)
        work_f = sb("work_f", [P, 7744])

        bank = [ctx.enter_context(nc.psum_tensor(f"bank{i}", [P, 512], f32)) for i in range(0)]
        psum = ctx.enter_context(nc.psum_tensor("psum", [P, 8, 512], f32))

        ident = const[:, 0:P]
        kone = const[:, P:P + 1]
        low0 = const[:, P + 1:P + 1 + E0 * E0]
        low1 = const[:, P + 1 + E0 * E0:CF - R]
        head_rows = const[:, CF - R:CF]
        bq0, bo0, bq1, bo1 = bias[:, 0:6], bias[:, 6:8], bias[:, 8:11], bias[:, 11:13]
        gate_b, route_b = bias[:, 13:13 + E1], bias[:, 13 + E1:13 + 2 * E1]

        def carve(tensor):
            at = [0]

            def take(*shape):
                n = 1
                for s in shape:
                    n *= s
                ap = tensor[:, at[0]:at[0] + n]
                at[0] += n
                if len(shape) == 2:
                    ap = ap.rearrange("p (a b) -> p a b", b=shape[1])
                if len(shape) == 3:
                    ap = ap.rearrange("p (a b c) -> p a b c", b=shape[1], c=shape[2])
                return ap
            return take

        def attention_weights(aw, nq, ng):
            take = carve(awr)
            a = [take(aw), take(aw)]
            q0, o0 = KH * ng, KH * ng + KH * nq
            return [(w[:, q0:o0].rearrange("p (k n) -> p k n", k=KH),
                     w[:, o0:aw].rearrange("p (k n) -> p k n", k=KH),
                     [w[:, k * ng:k * ng + P] for k in range(KH)]) for w in a], take
        (w0_hi, w0_lo), _ = attention_weights(AW0, 3 * H, E0)
        (w1_hi, w1_lo), take = attention_weights(AW1, H + 2 * NG * HD, E1 + 1)
        selq = take(2, 4, P)
        selk = take(2, NG, P)

        lt = work_f[:, 5632:5632 + T].rearrange("p (b t) -> p b t", b=B)
        tr, tf = carve(work_r), carve(work_f)
        qk_hi, qk_lo = tr(4, S), tr(4, S)
        v_hi, v_lo = tr(QT, H), tr(QT, H)
        p_hi, p_lo = tr(QT, S), tr(QT, S)
        c_hi, c_lo = tr(KH, S), tr(KH, S)
        vt = tf(KH, S)
        prob = tf(QT, S)
        sm = tf(4, QT)

        tr, tf = carve(work_r), carve(work_f)
        qc_hi, qc_lo = tr(KH, S), tr(KH, S)
        kc_hi, kc_lo = tr(S), tr(S)
        qs = [tr(S) for _ in range(2)]
        qm = [tr(S) for _ in range(2)]
        km = [tr(R, S) for _ in range(4)]
        mz = tr(QT, R, 32)
        kv = tf(S)
        va = tf(QT, NG, 32)
        pt = [tf(R, S) for _ in range(2)]
        ot = tf(S)
        mx = tf(2, QT * R)
        rec = tf(QT * R)
        ks = tf(S)

        tr = carve(work_r[:, 13824 - 2 * KH * T:13824])
        on_hi, on_lo = tr(KH, T), tr(KH, T)
        on = xn

        tf = carve(work_f)
        fw = []
        for nf in (NF0, NF1):
            tr = carve(work_r)
            fw.append((tr(nf, WS), tr(nf, WT)))
        tr = carve(work_r[:, NF0 * (WS + WT):13824])
        h_hi, h_lo = tr(4, S), tr(4, S)
        sg, su, hh = tf(2, S), tf(2, S), tf(2, S)
        at = KH * S + QT * S + 4 * QT
        cmp_a, cmp_b = (work_f[:, at + i * QT * E0 * E0:at + (i + 1) * QT * E0 * E0] for i in range(2))

        s_x, s_c = [sem(f"s_xin{b}") for b in range(B)], sem("s_c")
        s_lt, s_lx, s_zero, s_nm = (sem(n) for n in ("s_lt", "s_lx", "s_zero", "s_nm"))
        s_raw, s_split, s_wh = sem("s_raw"), sem("s_split"), sem("s_wh")
        s_dve, s_sq, s_ve = sem("s_dve"), sem("s_sq"), sem("s_ve")
        s_xn, s_xnT, s_xh, s_xl = sem("s_xn"), sem("s_xnT"), sem("s_xh"), sem("s_xl")
        s_lg, s_ex, s_exd = sem("s_lg"), sem("s_ex"), sem("s_exd")
        s_gw, s_gt, s_wt = sem("s_gw"), sem("s_gt"), sem("s_wt")
        s_lc, s_g0, s_g1 = sem("s_lc"), sem("s_g0"), sem("s_g1")
        a_pj, a_hi, a_lo, a_vt, a_vx = sem("a_pj"), sem("a_hi"), sem("a_lo"), sem("a_vt"), sem("a_vx")
        a_vh, a_vl, a_sc, a_m, a_n = sem("a_vh"), sem("a_vl"), sem("a_sc"), sem("a_m"), sem("a_n")
        a_e, a_r, a_p, a_pt, a_ph, a_pl = (sem(n) for n in ("a_e", "a_r", "a_p", "a_pt", "a_ph", "a_pl"))
        a_cx, a_ch, a_cl, a_o, a_y = (sem(n) for n in ("a_cx", "a_ch", "a_cl", "a_o", "a_y"))
        f_gu, f_s, f_p, f_h, f_hi, f_lo, f_dn, f_y = (
            [sem(f"{n}{i}") for i in range(2)] for n in ("f_gu", "f_s", "f_p", "f_h", "f_hi", "f_lo", "f_dn", "f_y"))
        s_yt, s_x1, s_out = sem("s_yt"), sem("s_x1"), sem("s_out")
        b_pj, b_kv, b_hi, b_lo, b_vt, b_va = (sem(n) for n in ("b_pj", "b_kv", "b_hi", "b_lo", "b_vt", "b_va"))
        b_sq, b_qs, b_sk, b_ks, b_sn, b_mx = (sem(n) for n in ("b_sq", "b_qs", "b_sk", "b_ks", "b_sn", "b_mx"))
        b_m1, b_m2, b_mt, b_qm, b_st, b_ex = (sem(n) for n in ("b_m1", "b_m2", "b_mt", "b_qm", "b_st", "b_ex"))
        b_km = sem("b_km")
        b_pv, b_ot, b_ox, b_rc, b_on, b_nt = (sem(n) for n in ("b_pv", "b_ot", "b_ox", "b_rc", "b_on", "b_nt"))
        b_nh, b_nl, b_o, b_y = (sem(n) for n in ("b_nh", "b_nl", "b_o", "b_y"))

        block = ctx.enter_context(nc.Block())

        SPLIT_A0 = 1
        SPLIT_F0 = SPLIT_A0
        SPLIT_A1 = SPLIT_F0 + G0 * NF0 + 1
        SPLIT_F1 = SPLIT_A1

        @block.sync
        def _(sp):
            for b in range(B):
                sp.dma_start(x[:, b * QT:(b + 1) * QT, :],
                             x_in[b * S:(b + 1) * S, :].rearrange("(t p) h -> p t h", p=P)).then_inc(s_x[b], 16)
            sp.dma_start(const[:], const_in).then_inc(s_c, 16)
            sp.dma_start(bias[:], bias_in).then_inc(s_c, 16)
            sp.dma_start(raw[:, 0:AW0], aw0_in).then_inc(s_raw, 16)
            with sp.Fori(0, G0) as g:
                sp.wait_ge(s_split, g * NF0 + SPLIT_F0)
                sp.dma_start(raw[:], ffn0_in[bass.ts(g, P), :]).then_inc(s_raw, 16)
            sp.wait_ge(s_split, SPLIT_F0 + G0 * NF0)
            sp.dma_start(raw[:, 0:AW1], aw1_in).then_inc(s_raw, 16)
            sp.dma_start(raw[:, AW1:AW1 + NSELQ + NSELK], sel_in).then_inc(s_raw, 16)
            with sp.Fori(0, G1) as g:
                sp.wait_ge(s_split, g * NF1 + SPLIT_F1)
                sp.dma_start(raw[:, 0:NF1 * WS], ffn1_in[bass.ts(g, P), :]).then_inc(s_raw, 16)
            for i in range(TT // 2):
                sp.wait_ge(s_x1, TT // 2 + i + 1)
                sp.dma_start(out[2 * i * P:(2 * i + 2) * P, :].rearrange("(t p) h -> p t h", p=P),
                             x[:, 2 * i:2 * i + 2, :]).then_inc(s_out, 16)
            sp.wait_ge(s_out, 16 * (TT // 2))

        @block.gpsimd
        def _(pool):
            nc.gpsimd.memset(zero[:], 0.0).then_inc(s_zero, 1)
            pool.wait_ge(s_zero, 1)

            def high(o, i):
                return nc.gpsimd.tensor_tensor(o, i, zero[:, 0:1].broadcast_to([P, i.shape[1]]), ALU.add)

            pool.wait_ge(s_raw, 16)
            high(awr[:, 0:AW0], raw[:, 0:AW0]).then_inc(s_wh, 1)
            pool.wait_ge(s_wh, 1)
            nc.gpsimd.tensor_tensor(awr[:, AW0:2 * AW0], raw[:, 0:AW0], awr[:, 0:AW0].bitcast(f32),
                                    ALU.subtract).then_inc(s_split, 1)
            nh = 1

            def split_tile(layer, f, wh):
                fw_hi, fw_lo = fw[layer]
                high(fw_hi[:, f, :], raw[:, f * WS:(f + 1) * WS]).then_inc(s_wh, 1)
                pool.wait_ge(s_wh, wh)
                nc.gpsimd.tensor_tensor(fw_lo[:, f, :], raw[:, f * WS:f * WS + WT],
                                        fw_hi[:, f, 0:WT].bitcast(f32), ALU.subtract).then_inc(s_split, 1)

            pool.wait_ge(s_raw, 2 * 16)
            pool.wait_ge(a_y, 2 * B + 1)
            for f in range(NF0):
                split_tile(0, f, 1 + f + 1)
            for g in range(1, G0):
                pool.wait_ge(s_raw, g * 16 + 2 * 16)
                for f in range(NF0):
                    pool.wait_ge(f_dn[0], g * (B * NF0) + (f + 1 - NF0))
                    split_tile(0, f, g * NF0 + (1 + f + 1))
            pool.wait_ge(s_raw, (G0 + 3) * 16)
            high(awr[:, 0:AW1], raw[:, 0:AW1]).then_inc(s_wh, 1)
            pool.wait_ge(s_wh, 1 + G0 * NF0 + 1)
            high(awr[:, 2 * AW1:2 * AW1 + NSELQ + NSELK], raw[:, AW1:AW1 + NSELQ + NSELK])
            nc.gpsimd.tensor_tensor(awr[:, AW1:2 * AW1], raw[:, 0:AW1], awr[:, 0:AW1].bitcast(f32),
                                    ALU.subtract).then_inc(s_split, 1)
            with pool.Fori(0, B) as b:
                for g in range(NG):
                    pool.wait_ge(b_ks, b * NG + (g + 1))
                    for r in range(R):
                        ins = nc.gpsimd.tensor_tensor(km[g % 4][:, r, :], ks, head_rows[:, r:r + 1].broadcast_to([P, S]),
                                                      ALU.mult)
                    ins.then_inc(b_km, 1)
            pool.wait_ge(s_raw, (G0 + 4) * 16)
            pool.wait_ge(b_pv, B * NG * QT)
            for f in range(NF1):
                if NF1 * WS + (f + 1) * WT > 13824 - 2 * KH * T:
                    pool.wait_ge(b_o, 2 * B)
                split_tile(1, f, 2 + G0 * NF0 + f + 1)
            for g in range(1, G1):
                pool.wait_ge(s_raw, g * 16 + (G0 + 4) * 16)
                for f in range(NF1):
                    pool.wait_ge(f_dn[1], g * (B * NF1) + (f + 1 - NF1))
                    split_tile(1, f, g * NF1 + (2 + G0 * NF0 + f + 1))

        @block.tensor
        def _(pe):
            def mm3(o, w_hi, w_lo, x_hi, x_lo, first, last):
                nc.tensor.matmul(o, w_hi, x_hi, start=first, stop=False)
                nc.tensor.matmul(o, w_hi, x_lo, start=False, stop=False)
                return nc.tensor.matmul(o, w_lo, x_hi, start=False, stop=last)

            def norm_and_logits(layer, whi, wlo, ne):
                for b in range(B):
                    pe.wait_ge(s_xn, layer * TT + (b + 1) * QT)
                    for k in range(KH):
                        for t in range(QT):
                            ins = nc.tensor.transpose(psum[:, 2 * b + k, t * P:(t + 1) * P],
                                                      xn[:, b * QT + t, k * P:(k + 1) * P], ident)
                        ins.then_inc(s_xnT, 1)
                pe.wait_ge(s_xl, (layer + 1) * 2 * B)
                pe.wait_ge(s_split, SPLIT_A1 if layer else SPLIT_A0)
                for b in range(B):
                    tok = slice(b * S, (b + 1) * S)
                    for k in range(KH):
                        ins = mm3(psum[:, b, :], whi[2][k], wlo[2][k], xt_hi[:, k, tok], xt_lo[:, k, tok],
                                  k == 0, k == KH - 1)
                    ins.then_inc(s_lg, 1)
                for b in range(B):
                    pe.wait_ge(s_lt, layer * B + b + 1)
                    for t in range(QT):
                        ins = nc.tensor.transpose(psum[:, 4 + b, t * P:(t + 1) * P], lt[:, b, t * P:(t + 1) * P], ident)
                ins.then_inc(s_lx, 1)

            def gating_transposes(layer, cols):
                pe.wait_ge(s_gw, B + layer)
                for t in range(TT):
                    ins = nc.tensor.transpose(psum[:, 4 + t // 4, (t % 4) * P:(t % 4 + 1) * P],
                                              gw[:, t * cols:t * cols + P].bitcast(f32), ident)
                ins.then_inc(s_gt, 1)
                pe.wait_ge(s_wt, layer + 1)

            def feed_forward(layer, nf, groups, split0):
                gu, h, lo, dn, yf = (s[layer] for s in (f_gu, f_h, f_lo, f_dn, f_y))
                fw_hi, fw_lo = fw[layer]
                nt = B * nf
                rows = LN_COLS1 if layer else LN_COLS

                def up(j, g, g_off):
                    k, f = j // nf, j % nf
                    pe.wait_ge(s_split, g * nf + (split0 + f + 1 + g_off * nf))
                    if not (isinstance(g, int) and j < 2):
                        pe.wait_ge(h, g * nt + (j - 1 + g_off * nt))
                    tok = slice(k * S, (k + 1) * S)
                    for c in range(2):
                        for i in range(KH):
                            col = (c * KH + i) * P
                            mm3(psum[:, 2 * c + j % 2, :], fw_hi[:, f, col:col + P], fw_lo[:, f, col:col + P],
                                xt_hi[:, i, tok], xt_lo[:, i, tok], i == 0, i == KH - 1)
                    nc.tensor.matmul(psum[:, 4 + j % 2, :], fw_hi[0:rows, f, WT:WS], wt[0:rows, tok],
                                     start=True, stop=True).then_inc(gu, 1)

                def down(j, g):
                    k, f = j // nf, j % nf
                    pe.wait_ge(lo, g * nt + (j + 1))
                    if f == 0:
                        pe.wait_ge(yf, g * B + (k + 1))
                    for c in range(KH):
                        col = WC + c * P
                        ins = mm3(psum[:, 6 + c, :], fw_hi[:, f, col:col + P], fw_lo[:, f, col:col + P],
                                  h_hi[:, j % 4, :], h_lo[:, j % 4, :], f == 0, f == nf - 1)
                    ins.then_inc(dn, 1)

                up(0, 0, 0)
                up(1, 0, 0)
                with pe.Fori(0, groups - 1) as g:
                    for j in range(nt):
                        if j + 2 < nt:
                            up(j + 2, g, 0)
                        else:
                            up(j + 2 - nt, g, 1)
                        down(j, g)
                for j in range(nt):
                    if j + 2 < nt:
                        up(j + 2, groups - 1, 0)
                    down(j, groups - 1)

            def sum_to_tokens(layer):
                pe.wait_ge(f_y[layer], (G1 if layer else G0) * B + 1)
                for t in range(TT):
                    for k in range(KH):
                        ins = nc.tensor.transpose(psum[:, t // 2, (t % 2) * H + k * P:(t % 2) * H + (k + 1) * P],
                                                  yacc[:, k, t * P:(t + 1) * P], ident)
                    if t % 2:
                        ins.then_inc(s_yt, 1)

            pe.wait_ge(s_c, 32)
            norm_and_logits(0, w0_hi, w0_lo, E0)

            def project0(n0, n1, b1, o0):
                for n in range(n0, n1):
                    for i in range(KH):
                        ins = mm3(psum[:, o0 + n - n0, :], w0_hi[0][:, i, n * P:(n + 1) * P], w0_lo[0][:, i, n * P:(n + 1) * P],
                                  xt_hi[:, i, bass.ts(b1, S)], xt_lo[:, i, bass.ts(b1, S)], i == 0, i == KH - 1)
                    ins.then_inc(a_pj, 1)

            def values_by_key0(b1):
                for t in range(QT):
                    for c in range(KH):
                        ins = nc.tensor.transpose(psum[:, 6 + t // 2, (t % 2) * H + c * P:(t % 2) * H + (c + 1) * P],
                                                  vt[:, c, t * P:(t + 1) * P], ident)
                    if t % 2:
                        ins.then_inc(a_vx, 1)

            def attention0(b, last):
                pe.wait_ge(a_lo, b * 4 + 4)
                for t in range(QT):
                    if t == 2:
                        pe.wait_ge(a_y, b * 2 + 1)
                    for i in range(KH):
                        q = slice(t * P, (t + 1) * P)
                        ins = mm3(psum[:, t, :], qk_hi[:, i, q], qk_lo[:, i, q], qk_hi[:, 2 + i, :],
                                  qk_lo[:, 2 + i, :], i == 0, i == KH - 1)
                    ins.then_inc(a_sc, 1)
                pe.wait_ge(a_vl, b * 2 + 2)
                if not last:
                    project0(0, 4, b + 1, 4)
                    pe.wait_ge(a_lo, b * 4 + 8)
                for t in range(QT):
                    pe.wait_ge(a_p, b * QT + (t + 1))
                    for c in range(QT):
                        ins = nc.tensor.transpose(psum[:, 4 + t, c * P:(c + 1) * P], prob[:, t, c * P:(c + 1) * P], ident)
                    ins.then_inc(a_pt, 1)
                if not last:
                    project0(4, 6, b + 1, 2)
                pe.wait_ge(a_pl, b * QT + QT)
                for c in range(KH):
                    for t in range(QT):
                        ins = mm3(psum[:, c, :], v_hi[:, t, c * P:(c + 1) * P], v_lo[:, t, c * P:(c + 1) * P],
                                  p_hi[:, t, :], p_lo[:, t, :], t == 0, t == QT - 1)
                    ins.then_inc(a_cx, 1)
                if not last:
                    pe.wait_ge(a_vt, b * 2 + 4)
                    values_by_key0(b + 1)
                pe.wait_ge(a_cl, b * 2 + 2)
                for c in range(KH):
                    for i in range(KH):
                        ins = mm3(psum[:, 2 + c, :], w0_hi[1][:, i, c * P:(c + 1) * P], w0_lo[1][:, i, c * P:(c + 1) * P],
                                  c_hi[:, i, :], c_lo[:, i, :], i == 0, i == KH - 1)
                    ins.then_inc(a_o, 1)

            project0(0, 4, 0, 0)
            pe.wait_ge(s_lc, 1)
            project0(4, 6, 0, 4)
            pe.wait_ge(a_vt, 2)
            values_by_key0(0)
            pe.wait_ge(a_lo, 4)
            with pe.Fori(0, B - 1) as b:
                attention0(b, False)
            attention0(B - 1, True)
            gating_transposes(0, LN_COLS)
            pe.wait_ge(a_y, 2 * B + 1)
            feed_forward(0, NF0, G0, SPLIT_F0)
            sum_to_tokens(0)
            norm_and_logits(1, w1_hi, w1_lo, E1 + 1)
            pe.wait_ge(s_lc, 3)
            NP, NQ = NG * QT * R, NG * QT

            def project(n, b1, o):
                for i in range(KH):
                    ins = mm3(o, w1_hi[0][:, i, n * P:(n + 1) * P], w1_lo[0][:, i, n * P:(n + 1) * P],
                              xt_hi[:, i, bass.ts(b1, S)], xt_lo[:, i, bass.ts(b1, S)], i == 0, i == KH - 1)
                ins.then_inc(b_pj, 1)

            def values_by_key(o):
                for t in range(QT):
                    ins = nc.tensor.transpose(o[:, t * P:(t + 1) * P], kv[:, t * P:(t + 1) * P], ident)
                ins.then_inc(b_vt, 1)

            def stack_q(g):
                nc.tensor.matmul(psum[:, 0, :], selq[:, 0, g % 4, :], qc_hi[:, g % NG // 4, :], start=True, stop=False)
                nc.tensor.matmul(psum[:, 0, :], selq[:, 1, g % 4, :], qc_lo[:, g % NG // 4, :],
                                 start=False, stop=True).then_inc(b_sq, 1)

            def stack_k(g):
                nc.tensor.matmul(psum[:, 0, :], selk[0:64, 0, g % NG, :], kc_hi[0:64, :], start=True, stop=False)
                nc.tensor.matmul(psum[:, 0, :], selk[0:64, 1, g % NG, :], kc_lo[0:64, :],
                                 start=False, stop=True).then_inc(b_sk, 1)

            def scores(b, g, i):
                if not (isinstance(b, int) and b * NG + g == 0 and i < 2):
                    pe.wait_ge(b_mx, b * NP + (g * QT * R + i - 1))
                t, r = i // R, i % R
                nc.tensor.matmul(psum[:, 1 + i % 2, :], qs[g % 2][:, t * P:(t + 1) * P],
                                 km[g % 4][:, r, :], start=True, stop=True).then_inc(b_sn, 1)

            def scores_t(b, g, i):
                t, h = i // 2, i % 2
                if g >= 1 or i >= 2:
                    pe.wait_ge(b_ex, b * (2 * NQ) + (g * 2 * QT + i - 1))
                for r in (2 * h, 2 * h + 1):
                    ins = nc.tensor.matmul(psum[:, 3 + 2 * h + r % 2, :], km[g % 4][:, r, t * P:(t + 1) * P],
                                           qm[g % 2], start=True, stop=True)
                ins.then_inc(b_st, 1)

            def values(b, g, t):
                pe.wait_ge(b_ex, b * (2 * NQ) + ((g * QT + t) * 2 + 2))
                if t == 0 and g >= 1:
                    pe.wait_ge(b_ot, b * NG + g)
                if t == 0 and g == 0:
                    pe.wait_ge(b_va, b + 1)
                for r in range(R):
                    ins = nc.tensor.matmul(psum[32 * r:32 * r + 32, 7, :], va[:, t, g, :], pt[t % 2][:, r, :],
                                           start=(t == 0), stop=(t == QT - 1), tile_position=(0, 32 * r))
                ins.then_inc(b_pv, 1)

            def outputs_t(b, g):
                pe.wait_ge(b_ot, b * NG + (g + 1))
                for t in range(QT):
                    ins = nc.tensor.transpose(psum[:, 0, t * P:(t + 1) * P], ot[:, t * P:(t + 1) * P], ident)
                ins.then_inc(b_ox, 1)

            def maxima_t(b, g):
                pe.wait_ge(b_m2, b * NG + (g + 1))
                for t in range(QT):
                    ins = nc.tensor.transpose(psum[:, 0, t * P:(t + 1) * P],
                                              mz[:, t].rearrange("p r c -> p (r c)").bitcast(f32), ident)
                ins.then_inc(b_mt, 1)

            TRANSPOSED = (0, 1, 3, 4, 8, 9, 12, 14)
            VALUED = (6, 10)

            def stage(b, s, last):
                front, back, stacks = not (last and s == NG), s >= 1, not (last and s >= NG - 1)
                following = not last and s >= 1
                for i in range(QT * R):
                    if i == 0:
                        if front:
                            pe.wait_ge(b_km, b * NG + (s + 1))
                    if front:
                        scores(b, s, i)
                    if i == 0 and back:
                        pe.wait_ge(b_qm, b * NG + s)
                    if back:
                        if i in TRANSPOSED:
                            scores_t(b, s - 1, TRANSPOSED.index(i))
                        if i in VALUED:
                            values(b, s - 1, VALUED.index(i))
                    if i == 2:
                        if s == 1:
                            pe.wait_ge(b_on, b * NG + 1)
                        if following and s == NG - 1:
                            project(2, b + 1, psum[:, 0, :])
                        elif stacks:
                            if s == 0:
                                pe.wait_ge(b_ks, 1)
                            stack_q(s + 1)
                    if i == 7:
                        if following and s == NG - 1:
                            pe.wait_ge(b_hi, b * 3 + 6)
                            stack_q(s + 1)
                        elif stacks:
                            pe.wait_ge(b_qs, b * NG + (s + 2))
                            stack_k(s + 1)
                    if i == 11:
                        if following and s == NG - 1:
                            pe.wait_ge(b_qs, b * NG + (s + 2))
                            pe.wait_ge(b_lo, b * 3 + 6)
                            stack_k(s + 1)
                        elif following and s in (NG - 3, NG - 2):
                            pe.wait_ge(b_ks, b * NG + (s + 2))
                            project(s - (NG - 3), b + 1, psum[:, 0, :])
                    if i == 13 and s >= 2:
                        if following and s in (NG - 3, NG - 2):
                            pe.wait_ge(b_lo, b * 3 + (s - (NG - 3) + 4))
                        elif stacks:
                            pe.wait_ge(b_ks, b * NG + (s + 2))
                        outputs_t(b, s - 2)
                if back:
                    values(b, s - 1, 2)
                if front:
                    if s >= 2:
                        pe.wait_ge(b_on, b * NG + s)
                    else:
                        pe.wait_ge(b_ks, b * NG + (s + 2))
                    maxima_t(b, s)
                if back:
                    values(b, s - 1, QT - 1)

            def sequence(b, last):
                for s in range(1, NG + 1):
                    stage(b, s, last)
                if last:
                    pe.wait_ge(b_on, b * NG + NG)
                else:
                    pe.wait_ge(b_qm, b * NG + (NG + 1))
                outputs_t(b, NG - 1)
                if not last:
                    pe.wait_ge(b_on, b * NG + (NG + 1))
                    values_by_key(psum[:, 0, :])

            for n in range(3):
                project(n, 0, psum[:, 1 + n, :])
            pe.wait_ge(b_kv, 1)
            values_by_key(psum[:, 4, :])
            pe.wait_ge(b_lo, 3)
            pe.wait_ge(b_va, 1)
            stack_q(0)
            pe.wait_ge(b_qs, 1)
            stack_k(0)
            stage(0, 0, False)
            with pe.Fori(0, B - 1) as b:
                sequence(b, False)
            sequence(B - 1, True)
            pe.wait_ge(b_on, B * NG + 1)
            for b in range(B):
                for k in range(KH):
                    for t in range(QT):
                        ins = nc.tensor.transpose(psum[:, 2 * b + k, t * P:(t + 1) * P],
                                                  on[:, b * QT + t, k * P:(k + 1) * P], ident)
                    ins.then_inc(b_nt, 1)
            for b in range(B):
                tok = slice(b * S, (b + 1) * S)
                pe.wait_ge(b_nl, 2 * b + 2)
                for c in range(KH):
                    for i in range(KH):
                        ins = mm3(psum[:, 2 * b + c, :], w1_hi[1][:, i, c * P:(c + 1) * P], w1_lo[1][:, i, c * P:(c + 1) * P],
                                  on_hi[:, i, tok], on_lo[:, i, tok], i == 0, i == KH - 1)
                    ins.then_inc(b_o, 1)
            pe.wait_ge(b_y, 2 * B)
            gating_transposes(1, LN_COLS1)
            feed_forward(1, NF1, G1, SPLIT_F1)
            sum_to_tokens(1)

        @block.scalar
        def _(act):
            def copy(o, i):
                return nc.scalar.copy(o, i)

            def norm(layer):
                def parts(b):
                    for k in range(KH):
                        act.wait_ge(s_xnT, layer * 2 * B + b * KH + k + 1)
                        copy(xt_hi[:, k, b * S:(b + 1) * S], psum[:, 2 * b + k, :]).then_inc(s_xh, 1)

                def normalised(b):
                    for t in range(b * QT, (b + 1) * QT):
                        nc.scalar.activation(xn[:, t, :], x[:, t, :], ACT.Identity, scale=rs[:, 4, t:t + 1],
                                             bias=rs[:, 7, t:t + 1]).then_inc(s_xn, 1)

                if layer == 0:
                    for b in range(B):
                        act.wait_ge(s_ve, b + 1)
                        nc.scalar.activation(rs[:, 1, b * QT:(b + 1) * QT], rs[:, 0, b * QT:(b + 1) * QT],
                                             ACT.Sqrt).then_inc(s_sq, 1)
                        if b >= 1:
                            parts(b - 1)
                        act.wait_ge(s_nm, b + 1)
                        normalised(b)
                else:
                    act.wait_ge(s_ve, B + 1)
                    nc.scalar.activation(rs[:, 1, :], rs[:, 0, :], ACT.Sqrt).then_inc(s_sq, 1)
                    act.wait_ge(s_nm, B + 1)
                    for b in range(B):
                        normalised(b)
                        if b >= 1:
                            parts(b - 1)
                parts(B - 1)

            def logits(layer):
                for b in range(B):
                    act.wait_ge(s_lg, layer * B + b + 1)
                    copy(lt[:, b, :], psum[:, b, :]).then_inc(s_lt, 1)

            def gating_exp(ne, count, n):
                act.wait_ge(s_ex, count)
                nc.scalar.activation(pr[:, 0:n, 0:ne], pr[:, 0:n, 0:ne], ACT.Exp).then_inc(s_exd, 1)

            def gating_weights(layer):
                act.wait_ge(s_gt, layer + 1)
                rows = LN_COLS1 if layer else LN_COLS
                copy(wt[0:rows, :].rearrange("p (a b) -> p a b", a=B), psum[0:rows, 4:8, :]).then_inc(s_wt, 1)

            def feed_forward(layer, nf, groups):
                gu, s, h, hi = (q[layer] for q in (f_gu, f_s, f_h, f_hi))
                nt = B * nf
                with act.Fori(0, groups) as g:
                    for j in range(nt):
                        act.wait_ge(gu, g * nt + (j + 1))
                        nc.scalar.activation(sg[:, j % 2, :], psum[:, j % 2, :], ACT.Silu).then_inc(s, 1)
                        act.wait_ge(h, g * nt + (j + 1))
                        copy(h_hi[:, j % 4, :], hh[:, j % 2, :]).then_inc(hi, 1)

            norm(0)
            logits(0)

            def projections(b1, o0):
                for n in range(4):
                    act.wait_ge(a_pj, b1 * 6 + (n + 1))
                    nc.scalar.activation(qk_hi[:, n, :], psum[:, o0 + n, :], ACT.Identity, bias=bq0[:, n:n + 1]).then_inc(a_hi, 1)

            def values_projected(b1, o0):
                for n in (4, 5):
                    act.wait_ge(a_pj, b1 * 6 + (n + 1))
                    nc.scalar.activation(vt[:, n - 4, :], psum[:, o0 + n - 4, :], ACT.Identity, bias=bq0[:, n:n + 1]).then_inc(a_vt, 1)

            def values_by_key0(b1):
                for c in range(2):
                    act.wait_ge(a_vx, b1 * 2 + (c + 1))
                    copy(v_hi[:, 2 * c:2 * c + 2, :], psum[:, 6 + c, :].rearrange("p (t h) -> p t h", h=H)).then_inc(a_vh, 1)

            def attention0(b, last):
                for t in range(QT):
                    act.wait_ge(a_n, b * QT + (t + 1))
                    nc.scalar.activation(prob[:, t, :], psum[:, t, :], ACT.Exp, scale=1.0 / 16.0, bias=sm[:, 1, t:t + 1],
                                         accum_out=sm[:, 2, t:t + 1]).then_inc(a_e, 1)
                if not last:
                    projections(b + 1, 4)
                for t in range(QT):
                    act.wait_ge(a_pt, b * QT + (t + 1))
                    copy(p_hi[:, :, t * P:(t + 1) * P], psum[:, 4 + t, :].rearrange("p (c q) -> p c q", q=P)).then_inc(a_ph, 1)
                gating_exp(E0, b + 1, QT)
                if not last:
                    values_projected(b + 1, 2)
                for c in range(KH):
                    act.wait_ge(a_cx, b * 2 + (c + 1))
                    copy(c_hi[:, c, :], psum[:, c, :]).then_inc(a_ch, 1)
                if not last:
                    values_by_key0(b + 1)
                for c in range(KH):
                    act.wait_ge(a_o, b * 2 + (c + 1))
                    nc.scalar.activation(yacc[:, c, bass.ts(b, S)], psum[:, 2 + c, :], ACT.Identity,
                                         bias=bo0[:, c:c + 1]).then_inc(a_y, 1)

            nc.scalar.copy(rs[:, 5, 0:1], rs[:, 4, 0:1]).then_inc(a_y, 1)
            projections(0, 0)
            values_projected(0, 4)
            values_by_key0(0)
            with act.Fori(0, B - 1) as b:
                attention0(b, False)
            attention0(B - 1, True)
            gating_weights(0)
            feed_forward(0, NF0, G0)
            norm(1)
            logits(1)

            def compact(n, b1, o):
                act.wait_ge(b_pj, b1 * 3 + (n + 1))
                if n < 2:
                    nc.scalar.activation(qc_hi[:, n, :], o, ACT.Identity, bias=bq1[:, n:n + 1]).then_inc(b_hi, 1)
                else:
                    nc.scalar.activation(kv[:], o, ACT.Identity, bias=bq1[:, 2:3]).then_inc(b_kv, 1)
                    nc.scalar.activation(kc_hi[:], o, ACT.Identity, bias=bq1[:, 2:3]).then_inc(b_hi, 1)

            def stack_q(b, g):
                act.wait_ge(b_sq, b * NG + (g + 1))
                copy(qs[g % 2], psum[:, 0, :]).then_inc(b_qs, 1)

            def stack_k(b, g):
                act.wait_ge(b_sk, b * NG + (g + 1))
                if g >= 1:
                    act.wait_ge(b_km, b * NG + g)
                nc.scalar.activation(ks, psum[:, 0, :], ACT.Identity, bias=kone).then_inc(b_ks, 1)

            def stage(b, s, last):
                back, stacks = s >= 1, not (last and s >= NG - 1)
                following = not last and s >= 1
                for t in range(QT):
                    if back:
                        g = s - 1
                        for h in range(2):
                            act.wait_ge(b_st, b * (2 * NG * QT) + ((g * QT + t) * 2 + h + 1))
                            if g * QT + t >= 2:
                                act.wait_ge(b_pv, b * (NG * QT) + (g * QT + t - 1))
                            nc.scalar.activation(pt[t % 2][:, 2 * h:2 * h + 2, :], psum[:, 3 + 2 * h:5 + 2 * h, :],
                                                 ACT.Exp, scale=float(HD) ** -0.5).then_inc(b_ex, 1)
                    if following and s == NG - 1:
                        if t == 0:
                            compact(2, b + 1, psum[:, 0, :])
                        if t == 1:
                            stack_q(b, s + 1)
                        if t == 2:
                            stack_k(b, s + 1)
                    elif stacks:
                        if t == 0:
                            stack_q(b, s + 1)
                        if t == 1:
                            stack_k(b, s + 1)
                        if t == 2 and following and s in (NG - 3, NG - 2):
                            compact(s - (NG - 3), b + 1, psum[:, 0, :])
                if back:
                    act.wait_ge(b_pv, b * (NG * QT) + s * QT)
                    if s >= 2:
                        act.wait_ge(b_ox, b * NG + (s - 1))
                    copy(ot[:], psum[:, 7, :]).then_inc(b_ot, 1)

            for n in range(3):
                compact(n, 0, psum[:, 1 + n, :])
            stack_q(0, 0)
            stack_k(0, 0)
            stage(0, 0, False)
            with act.Fori(0, B - 1) as b:
                for s in range(1, NG + 1):
                    stage(b, s, False)
            for s in range(1, NG + 1):
                stage(B - 1, s, True)
            for n in range(2 * B):
                act.wait_ge(b_nt, n + 1)
                b, k = n // KH, n % KH
                copy(on_hi[:, k, b * S:(b + 1) * S], psum[:, n, :]).then_inc(b_nh, 1)
            for n in range(2 * B):
                act.wait_ge(b_o, n + 1)
                b, c = n // KH, n % KH
                nc.scalar.activation(yacc[:, c, b * S:(b + 1) * S], psum[:, n, :], ACT.Identity,
                                     bias=bo1[:, c:c + 1]).then_inc(b_y, 1)
            gating_exp(E1, B + 1, TT)
            gating_weights(1)
            feed_forward(1, NF1, G1)

        @block.vector
        def _(dve):
            v = nc.vector
            done = [0]

            def then(ins):
                done[0] += 1
                ins.then_inc(s_dve, 1)
                dve.wait_ge(s_dve, done[0])

            def norm(layer, ne):
                def statistics(b):
                    tiles = range(b * QT, (b + 1) * QT)
                    if layer == 0:
                        dve.wait_ge(s_x[b], 16)
                    for t in tiles:
                        ins = v.bn_stats(st[:, t, :], x[:, t, :])
                    then(ins)
                    for t in tiles:
                        ins = v.bn_aggr(mv[:, t, :], st[:, t, :])
                    then(ins)

                def normalised(n0, n1, count):
                    ve, sd, r0, t1, rstd = (rs[:, i, n0:n1] for i in range(5))
                    dve.wait_ge(s_sq, count)
                    then(v.reciprocal(r0, sd))
                    then(v.tensor_tensor(t1, r0, r0, ALU.mult))
                    then(v.tensor_tensor(t1, t1, ve, ALU.mult))
                    then(v.tensor_scalar(t1, t1, -0.5, 1.5, ALU.mult, ALU.add))
                    then(v.tensor_tensor(rstd, r0, t1, ALU.mult))
                    v.scalar_tensor_tensor(out=rs[:, 7, n0:n1], in0=mv[:, n0:n1, 0], scalar=-1.0, in1=rstd,
                                           op0=ALU.mult, op1=ALU.mult).then_inc(s_nm, 1)

                def parts(b):
                    for k in range(KH):
                        dve.wait_ge(s_xh, layer * 2 * B + b * KH + k + 1)
                        tok = slice(b * S, (b + 1) * S)
                        v.tensor_tensor(xt_lo[:, k, tok], psum[:, 2 * b + k, :], xt_hi[:, k, tok].bitcast(f32),
                                        ALU.subtract).then_inc(s_xl, 1)

                if layer == 0:
                    for b in range(B):
                        statistics(b)
                        v.tensor_scalar_add(rs[:, 0, b * QT:(b + 1) * QT], mv[:, b * QT:(b + 1) * QT, 1], EPS).then_inc(s_ve, 1)
                        normalised(b * QT, (b + 1) * QT, b + 1)
                        if b >= 1:
                            parts(b - 1)
                else:
                    for b in range(B):
                        residual(0, b)
                        dve.wait_ge(s_x1, (b + 1) * 2)
                        statistics(b)
                    v.tensor_scalar_add(rs[:, 0, :], mv[:, :, 1], EPS).then_inc(s_ve, 1)
                    normalised(0, TT, B + 1)
                    for b in range(B - 1):
                        parts(b)
                parts(B - 1)
                dve.wait_ge(s_lx, layer + 1)
                logits = psum[:, 4:8, :].rearrange("p b (t e) -> p (b t) e", e=P)[:, :, 0:ne]
                if layer == 0:
                    v.tensor_copy(lg[:, :, 0:ne], logits).then_inc(s_lc, 1)
                else:
                    v.tensor_tensor(lg[:, :, 0:ne], logits, gate_b.unsqueeze(1).broadcast_to([P, TT, ne]),
                                    ALU.add).then_inc(s_lc, 1)
                ne1 = ne + 1
                then(v.memset(gw[:].bitcast(mybir.dt.uint32), 0))
                v.memset(gw[:, 0:TT * 2 * ne1].rearrange("p (t c) -> p t c", c=2 * ne1)[:, :, ne:ne1].bitcast(f32),
                         1.0).then_inc(s_lc, 1)
                dve.wait_ge(s_lc, 2 * layer + 2)

            def gating(layer, ne, top, count, tiles, n, chain, base):
                step = [0]
                assert layer == 1 or n == QT

                def then(ins):
                    step[0] += 1
                    ins.then_inc(chain, 1)
                    dve.wait_ge(chain, base + step[0])

                ne1 = ne + 1
                l, p, rk = lg[:, tiles, 0:ne], pr[:, 0:n, 0:ne], rank[:, 0:n, 0:ne]
                if layer == 0:
                    l = rank[:, QT:2 * QT, 0:ne]
                sm5, sm6, sm7 = (rs[:, i, 0:n] for i in (5, 6, 7))
                col = lambda c: c.unsqueeze(2).broadcast_to([P, n, ne])

                def exponents():
                    if layer == 0:
                        then(v.tensor_copy(l, lg[:, tiles, 0:ne]))
                    then(v.reduce_max(sm5, l, AX.X))
                    v.tensor_tensor(p, l, col(sm5), ALU.subtract).then_inc(s_ex, 1)

                def weights():
                    dve.wait_ge(s_exd, count)
                    then(v.reduce_sum(sm6, p, AX.X))
                    then(v.reciprocal(sm7, sm6))
                    then(v.tensor_tensor(p, p, col(sm7), ALU.mult))
                    ca, cb = (c[:, 0:n * ne * ne].rearrange("p (t a b) -> p t a b", a=ne, b=ne) for c in (cmp_a, cmp_b))
                    if layer == 1:
                        then(v.tensor_tensor(l, p, route_b.unsqueeze(1).broadcast_to([P, n, ne]), ALU.add))
                    low = (low0, low1)[layer].rearrange("p (a b) -> p a b", b=ne).unsqueeze(1).broadcast_to([P, n, ne, ne])
                    other = l.unsqueeze(2).broadcast_to([P, n, ne, ne])
                    own = l.unsqueeze(3).broadcast_to([P, n, ne, ne])
                    v.tensor_tensor(ca, other, own, ALU.is_gt)
                    then(v.tensor_tensor(cb, other, own, ALU.is_equal))
                    then(v.tensor_tensor(cb, cb, low, ALU.mult))
                    then(v.tensor_tensor(ca, ca, cb, ALU.add))
                    then(v.tensor_reduce(rk, ca, AX.X, ALU.add))
                    then(v.tensor_scalar(rk, rk, float(top), None, ALU.is_lt))
                    then(v.tensor_tensor(p, p, rk, ALU.mult))
                    if layer == 1:
                        then(v.reduce_sum(sm6, p, AX.X))
                        then(v.reciprocal(sm7, sm6))
                        then(v.tensor_tensor(p, p, col(sm7), ALU.mult))
                    g = gw[:, 0:TT * 2 * ne1].rearrange("p (t c) -> p t c", c=2 * ne1)[:, tiles, :]
                    then(v.tensor_scalar(g[:, :, 0:ne], p, 1.0, None, ALU.mult))
                    v.tensor_tensor(g[:, :, ne1:ne1 + ne], p, g[:, :, 0:ne].bitcast(f32), ALU.subtract).then_inc(s_gw, 1)
                    return step[0]

                return exponents, weights

            def feed_forward(layer, nf, groups):
                gu, s, sp_, h, hi, lo, dn, yf = (q[layer] for q in (f_gu, f_s, f_p, f_h, f_hi, f_lo, f_dn, f_y))
                nt = B * nf
                v.memset(rs[:, 7, 0:1], 0.0).then_inc(yf, 1)
                def add_outputs(g, k):
                    dve.wait_ge(dn, g * nt + (k + 1) * nf)
                    tok = slice(k * S, (k + 1) * S)
                    v.tensor_tensor(yacc[:, :, tok], yacc[:, :, tok], psum[:, 6:8, :], ALU.add).then_inc(yf, 1)

                def group(g, first):
                    for j in range(nt):
                        dve.wait_ge(s, g * nt + (j + 1))
                        v.tensor_tensor(su[:, j % 2, :], sg[:, j % 2, :], psum[:, 2 + j % 2, :], ALU.mult).then_inc(sp_, 1)
                        dve.wait_ge(sp_, g * nt + (j + 1))
                        v.tensor_tensor(hh[:, j % 2, :], su[:, j % 2, :], psum[:, 4 + j % 2, :], ALU.mult).then_inc(h, 1)
                        dve.wait_ge(hi, g * nt + (j + 1))
                        v.tensor_tensor(h_lo[:, j % 4, :], hh[:, j % 2, :], h_hi[:, j % 4, :].bitcast(f32),
                                        ALU.subtract).then_inc(lo, 1)
                        if j % nf == 1 and (j > nf or not first):
                            if j > nf:
                                add_outputs(g, j // nf - 1)
                            else:
                                dve.wait_ge(dn, g * nt)
                                v.tensor_tensor(yacc[:, :, T - S:T], yacc[:, :, T - S:T], psum[:, 6:8, :],
                                                ALU.add).then_inc(yf, 1)

                group(0, True)
                with dve.Fori(1, groups) as g:
                    group(g, False)
                add_outputs(groups - 1, B - 1)

            def residual(layer, b):
                for i in range(b * QT // 2, (b + 1) * QT // 2):
                    dve.wait_ge(s_yt, layer * (TT // 2) + i + 1)
                    v.tensor_tensor(x[:, 2 * i:2 * i + 2, :], x[:, 2 * i:2 * i + 2, :],
                                    psum[:, i, :].rearrange("p (t h) -> p t h", h=H), ALU.add).then_inc(s_x1, 1)

            dve.wait_ge(s_c, 32)
            norm(0, E0)

            def projections(b1, o0):
                for n in range(4):
                    dve.wait_ge(a_hi, b1 * 4 + (n + 1))
                    v.scalar_tensor_tensor(out=qk_lo[:, n, :], in0=psum[:, o0 + n, :], scalar=bq0[:, n:n + 1],
                                           in1=qk_hi[:, n, :].bitcast(f32), op0=ALU.add, op1=ALU.subtract).then_inc(a_lo, 1)

            def values_by_key0(b1):
                for c in range(2):
                    dve.wait_ge(a_vh, b1 * 2 + (c + 1))
                    v.tensor_tensor(v_lo[:, 2 * c:2 * c + 2, :], psum[:, 6 + c, :].rearrange("p (t h) -> p t h", h=H),
                                    v_hi[:, 2 * c:2 * c + 2, :].bitcast(f32), ALU.subtract).then_inc(a_vl, 1)

            def attention0(b, last):
                for t in range(QT):
                    dve.wait_ge(a_sc, b * QT + (t + 1))
                    v.reduce_max(sm[:, 0, t:t + 1], psum[:, t, :], AX.X).then_inc(a_m, 1)
                    dve.wait_ge(a_m, b * QT + (t + 1))
                    v.tensor_scalar(sm[:, 1, t:t + 1], sm[:, 0, t:t + 1], -1.0 / 16.0, None, ALU.mult).then_inc(a_n, 1)
                for t in range(QT):
                    dve.wait_ge(a_e, b * QT + (t + 1))
                    v.reciprocal(sm[:, 3, t:t + 1], sm[:, 2, t:t + 1]).then_inc(a_r, 1)
                    dve.wait_ge(a_r, b * QT + (t + 1))
                    v.tensor_scalar(prob[:, t, :], prob[:, t, :], sm[:, 3, t:t + 1], None, ALU.mult).then_inc(a_p, 1)
                if not last:
                    projections(b + 1, 4)
                exponents, weights = gating(0, E0, TOP0, b + 1, bass.ts(b, QT), QT, s_g0, b * GATE_STEPS)
                exponents()
                for t in range(QT):
                    dve.wait_ge(a_ph, b * QT + (t + 1))
                    q = slice(t * P, (t + 1) * P)
                    v.tensor_tensor(p_lo[:, :, q], psum[:, 4 + t, :].rearrange("p (c q) -> p c q", q=P),
                                    p_hi[:, :, q].bitcast(f32), ALU.subtract).then_inc(a_pl, 1)
                steps = weights()
                assert steps == GATE_STEPS, steps
                for c in range(KH):
                    dve.wait_ge(a_ch, b * 2 + (c + 1))
                    v.tensor_tensor(c_lo[:, c, :], psum[:, c, :], c_hi[:, c, :].bitcast(f32), ALU.subtract).then_inc(a_cl, 1)
                if not last:
                    values_by_key0(b + 1)

            projections(0, 0)
            values_by_key0(0)
            with dve.Fori(0, B - 1) as b:
                attention0(b, False)
            attention0(B - 1, True)
            feed_forward(0, NF0, G0)
            norm(1, E1)
            then(v.memset(va[:], 0.0))
            v.memset(va[:, :, :, HD:HD + 1], 1.0)
            then(v.memset(mz[:].bitcast(mybir.dt.uint32), 0))
            NP = NG * QT * R

            def compact(n, b1, o):
                dve.wait_ge(b_hi, b1 * 3 + (n + 1))
                if n < 2:
                    v.scalar_tensor_tensor(out=qc_lo[:, n, :], in0=o, scalar=bq1[:, n:n + 1],
                                           in1=qc_hi[:, n, :].bitcast(f32), op0=ALU.add, op1=ALU.subtract).then_inc(b_lo, 1)
                else:
                    v.tensor_tensor(kc_lo[:], kv[:], kc_hi[:].bitcast(f32), ALU.subtract).then_inc(b_lo, 1)

            def values_by_key(b1, o):
                dve.wait_ge(b_vt, b1 + 1)
                v.tensor_copy(va[:, :, :, 0:HD], o.rearrange("p (t c) -> p t c", c=P)[:, :, 64:128]
                              .rearrange("p t (g d) -> p t g d", d=HD)).then_inc(b_va, 1)

            def normalise(b, g):
                dve.wait_ge(b_ox, b * NG + (g + 1))
                o = psum[:, 0, :].rearrange("p (q c) -> p q c", c=32)
                v.reciprocal(rec[:].unsqueeze(2), o[:, :, HD:HD + 1]).then_inc(b_rc, 1)
                dve.wait_ge(b_rc, b * NG + (g + 1))
                v.tensor_tensor(on[:, bass.ts(b, QT), g * 32:(g + 1) * 32].rearrange("p t (r d) -> p t r d", d=HD),
                                o[:, :, 0:HD].rearrange("p (t r) d -> p t r d", r=R),
                                rec[:].rearrange("p (t r) -> p t r", r=R).unsqueeze(3).broadcast_to([P, QT, R, HD]),
                                ALU.mult).then_inc(b_on, 1)

            def stage(b, s, last):
                front, following = not (last and s == NG), not last and s >= 1
                for i in range(QT * R):
                    if front:
                        dve.wait_ge(b_sn, b * NP + (s * QT * R + i + 1))
                        v.reduce_max(mx[:, s % 2, i:i + 1], psum[:, 1 + i % 2, :], AX.X).then_inc(b_mx, 1)
                    if following and i == 4 and s == NG - 1:
                        compact(2, b + 1, psum[:, 0, :])
                    if following and i == 12 and s in (NG - 3, NG - 2):
                        compact(s - (NG - 3), b + 1, psum[:, 0, :])
                    if i == (14 if front else 15) and s >= 2:
                        normalise(b, s - 2)
                if front:
                    dve.wait_ge(b_mx, b * NP + (s + 1) * QT * R)
                    if s >= 1:
                        dve.wait_ge(b_mt, b * NG + s)
                    m = mx[:, s % 2, :].unsqueeze(2)
                    z = mz[:].rearrange("p t r c -> p (t r) c")
                    v.tensor_scalar(z[:, :, 24:25], m, -1.0, None, ALU.mult).then_inc(b_m1, 1)
                    dve.wait_ge(b_m1, b * NG + (s + 1))
                    v.scalar_tensor_tensor(out=z[:, :, 25:26], in0=m, scalar=-1.0, in1=z[:, :, 24:25].bitcast(f32),
                                           op0=ALU.mult, op1=ALU.subtract).then_inc(b_m2, 1)
                    dve.wait_ge(b_mt, b * NG + (s + 1))
                    v.tensor_tensor(qm[s % 2], psum[:, 0, :], qs[s % 2].bitcast(f32), ALU.add).then_inc(b_qm, 1)

            for n in range(3):
                compact(n, 0, psum[:, 1 + n, :])
            v.memset(rec[:], 0.0).then_inc(b_on, 1)
            values_by_key(0, psum[:, 4, :])
            stage(0, 0, False)
            with dve.Fori(0, B - 1) as b:
                for s in range(1, NG + 1):
                    stage(b, s, False)
                normalise(b, NG - 1)
                values_by_key(b + 1, psum[:, 0, :])
            for s in range(1, NG + 1):
                stage(B - 1, s, True)
            normalise(B - 1, NG - 1)
            for n in range(2 * B):
                dve.wait_ge(b_nh, n + 1)
                b, k = n // KH, n % KH
                v.tensor_tensor(on_lo[:, k, b * S:(b + 1) * S], psum[:, n, :], on_hi[:, k, b * S:(b + 1) * S].bitcast(f32),
                                ALU.subtract).then_inc(b_nl, 1)
            exponents, weights = gating(1, E1, TOP1, B + 1, slice(0, TT), TT, s_g1, 0)
            exponents()
            weights()
            feed_forward(1, NF1, G1)
            for b in range(B):
                residual(1, b)


def kernel(**inputs):
    import numpy as np
    import concourse.bacc as bacc
    from concourse.bass_utils import run_bass_kernel_spmd

    a = {k: np.ascontiguousarray(v) for k, v in inputs.items()}
    zeros = lambda *s: np.zeros(s, np.float32)

    def halves(w):
        return w.reshape(KH, P, -1).transpose(1, 0, 2).reshape(P, -1)

    def columns(vec):
        return vec.reshape(-1, P).T

    aw0 = np.concatenate([halves(a["L0_ffn_gate_weight"].T), halves(a["L0_attn_w_qkv"].T),
                          halves(a["L0_attn_w_out"].T)], 1)
    gate1 = np.concatenate([a["L1_ffn_gate_w"], zeros(H, 1)], 1)
    aw1 = np.concatenate([halves(gate1), halves(a["L1_attn_w_qkv"].T), halves(a["L1_attn_w_out"].T)], 1)

    def ffn(gate, up, down, groups, nf, hidden_expert, experts):
        tiles = groups * nf
        out = zeros(groups, P, nf, WS)
        for n in range(tiles):
            g, f = n // nf, n % nf
            c = slice(n * P, (n + 1) * P)
            out[g, :, f, 0:KH * P] = halves(gate[:, c])
            out[g, :, f, KH * P:WC] = halves(up[:, c])
            out[g, :, f, WC:WT] = down[c]
            for r in range(P):
                e = hidden_expert(n * P + r)
                out[g, e, f, WT + r] = 1.0
                out[g, experts + 1 + e, f, WT + r] = 1.0
        return out.reshape(groups * P, nf * WS)

    def wide(w):
        return w.transpose(1, 0, 2).reshape(H, -1)

    pad = G0 * NF0 * P - E0 * F0 - FS0
    ffn0 = ffn(np.concatenate([wide(a["L0_ffn_w_gate"]), a["L0_ffn_ws_gate"], zeros(H, pad)], 1),
               np.concatenate([wide(a["L0_ffn_w_up"]), a["L0_ffn_ws_up"], zeros(H, pad)], 1),
               np.concatenate([a["L0_ffn_w_down"].reshape(-1, H), a["L0_ffn_ws_down"], zeros(pad, H)], 0),
               G0, NF0, lambda i: min(i // F0, E0), E0)
    ffn1 = ffn(np.concatenate([wide(a["L1_ffn_W1"]), a["L1_ffn_Ws1"]], 1),
               np.concatenate([wide(a["L1_ffn_Wg"]), a["L1_ffn_Wsg"]], 1),
               np.concatenate([a["L1_ffn_W2"].reshape(-1, H), a["L1_ffn_Ws2"]], 0),
               G1, NF1, lambda i: i // F1, E1)

    selq, selk = zeros(P, 2, 4, P), zeros(P, 2, NG, P)
    for r in range(R):
        for d in range(HD):
            for slot, part in enumerate((0, 0, 1)):
                for j in range(4):
                    selq[j * 32 + r * HD + d, part, j, 32 * r + slot * HD + d] = 1.0
            for slot, part in enumerate((0, 1, 0)):
                for g in range(NG):
                    selk[g * HD + d, part, g, 32 * r + slot * HD + d] = 1.0
    sel = np.concatenate([selq.reshape(P, -1), selk.reshape(P, -1)], 1)
    const = zeros(P, CF)
    const[:, 0:P] = np.eye(P, dtype=np.float32)
    for r in range(R):
        const[32 * r:32 * r + 32, CF - R + r] = 1.0
        const[32 * r + 3 * HD:32 * r + 3 * HD + 2, P] = 1.0
    for e in range(E0):
        const[:, P + 1 + e * E0:P + 1 + e * E0 + e] = 1.0
    for e in range(E1):
        const[:, P + 1 + E0 * E0 + e * E1:P + 1 + E0 * E0 + e * E1 + e] = 1.0
    bias = np.concatenate([columns(a["L0_attn_b_qkv"]), columns(a["L0_attn_b_out"]),
                           columns(a["L1_attn_b_qkv"]), columns(a["L1_attn_b_out"]),
                           np.broadcast_to(a["L1_ffn_gate_b"], (P, E1)),
                           np.broadcast_to(a["L1_ffn_biases"], (P, E1))], 1)

    host = {"x": a["L0_attn_hidden_states"].reshape(T, H), "aw0": aw0, "aw1": aw1, "sel": sel,
            "ffn0": ffn0, "ffn1": ffn1, "const": const, "bias": bias}
    nc = bacc.Bacc("TRN2", target_bir_lowering=False, num_devices=1)
    arrays, args = {}, []
    for name, value in host.items():
        arrays[f"in_{name}"] = np.ascontiguousarray(value)
        args.append(nc.dram_tensor(f"in_{name}", value.shape, mybir.dt.float32, kind="ExternalInput").ap())
    args.append(nc.dram_tensor("out_0", (T, H), mybir.dt.float32, kind="ExternalOutput").ap())
    program(nc, *args)
    r = run_bass_kernel_spmd(nc, [arrays], core_ids=[0])
    return r.results[0]["out_0"].reshape(B, S, H)
```

```python
import concourse.bass as bass
from concourse import mybir
from contextlib import ExitStack

P = 128
B, S, H = 4, 512, 256
T = B * S
TT = T // P
KH = H // P
QT = S // P
E0, TOP0, F0, FS0 = 16, 4, 176, 352
E1, TOP1, F1 = 7, 3, 256
NF0, G0 = 5, 5
NF1, G1 = 4, 4
WC = 2 * KH * P
WT = WC + H
WS = WT + P
NG, R, HD = 8, 4, 8
EPS = 1e-5
LN_COLS = 2 * (E0 + 1)
LN_COLS1 = 2 * (E1 + 1)
AW0 = KH * 3 * H + KH * H + KH * E0
AW1 = KH * (H + 2 * NG * HD) + KH * H + KH * (E1 + 1)
NSELQ = 2 * 4 * P
NSELK = 2 * NG * P
GATE_STEPS = 12
CF = P + 1 + E0 * E0 + E1 * E1 + R
BF = 6 + 3 + 2 * E1 + 2 * H


def program(nc, x_in, aw0_in, aw1_in, sel_in, ffn0_in, ffn1_in, const_in, bias_in, out):
    f32, f32r = mybir.dt.float32, mybir.dt.float32r
    ALU, ACT, AX = mybir.AluOpType, mybir.ActivationFunctionType, mybir.AxisListType
    ctx = ExitStack()
    with ctx:
        def sb(name, shape, dt=f32):
            return ctx.enter_context(nc.sbuf_tensor(name, shape, dt))

        def sem(name):
            return ctx.enter_context(nc.semaphore(name))

        x = sb("x", [P, TT, H])
        xn = sb("xn", [P, TT, H])
        xt_hi = sb("xt_hi", [P, KH, T], f32r)
        xt_lo = sb("xt_lo", [P, KH, T], f32r)
        wt = sb("wt", [P, T], f32r)
        raw = sb("raw", [P, NF0 * WS])
        awr = sb("awr", [P, max(2 * AW0, 2 * AW1 + NSELQ + NSELK)], f32r)
        const = sb("const", [P, CF])
        bias = sb("bias", [P, BF])
        st = sb("st", [P, TT, 6])
        mv = sb("mv", [P, TT, 2])
        zero = sb("zero", [P, 2])
        rs = sb("rs", [P, 8, TT])
        lg = sb("lg", [P, TT, E0])
        pr = sb("pr", [P, TT, E0])
        rank = sb("rank", [P, TT, E0])
        gw = sb("gw", [P, TT * LN_COLS + P], f32r)
        work_r = sb("work_r", [P, 13824], f32r)
        work_f = sb("work_f", [P, 7760])

        psum = ctx.enter_context(nc.psum_tensor("psum", [P, 8, 512], f32))

        ident = const[:, 0:P]
        kone = const[:, P:P + 1]
        low0 = const[:, P + 1:P + 1 + E0 * E0]
        low1 = const[:, P + 1 + E0 * E0:CF - R]
        head_rows = const[:, CF - R:CF]
        bq0, bq1 = bias[:, 0:6], bias[:, 6:9]
        gate_b, route_b = bias[:, 9:9 + E1], bias[:, 9 + E1:9 + 2 * E1]
        bo = [bias[:, BF - (2 - i) * H:BF - (1 - i) * H] for i in range(2)]

        def carve(tensor):
            at = [0]

            def take(*shape):
                n = 1
                for s in shape:
                    n *= s
                ap = tensor[:, at[0]:at[0] + n]
                at[0] += n
                if len(shape) == 2:
                    ap = ap.rearrange("p (a b) -> p a b", b=shape[1])
                if len(shape) == 3:
                    ap = ap.rearrange("p (a b c) -> p a b c", b=shape[1], c=shape[2])
                return ap
            return take

        def attention_weights(aw, nq, ng):
            take = carve(awr)
            a = [take(aw), take(aw)]
            q0, o0 = KH * ng, KH * ng + KH * nq
            return [(w[:, q0:o0].rearrange("p (k n) -> p k n", k=KH),
                     w[:, o0:aw].rearrange("p (k n) -> p k n", k=KH),
                     [w[:, k * ng:k * ng + P] for k in range(KH)]) for w in a], take
        (w0_hi, w0_lo), _ = attention_weights(AW0, 3 * H, E0)
        (w1_hi, w1_lo), take = attention_weights(AW1, H + 2 * NG * HD, E1 + 1)
        selq = take(2, 4, P)
        selk = take(2, NG, P)

        lt = [work_f[:, at:at + T].rearrange("p (b t) -> p b t", b=B) for at in (5632, 1536)]
        tr, tf = carve(work_r), carve(work_f)
        qk_hi, qk_lo = tr(4, S), tr(4, S)
        v_hi, v_lo = tr(QT, H), tr(QT, H)
        p_hi, p_lo = tr(QT, S), tr(QT, S)
        c_hi, c_lo = tr(KH, S), tr(KH, S)
        vt = tf(KH, S)
        prob = tf(QT, S)
        sm = tf(4, QT)

        tr, tf = carve(work_r), carve(work_f)
        qc_hi, qc_lo = tr(KH, S), tr(KH, S)
        kc_hi, kc_lo = tr(S), tr(S)
        qs = [tr(S) for _ in range(2)]
        qm = [tr(S) for _ in range(2)]
        km = [tr(R, S) for _ in range(4)]
        mz = tr(QT, R, 32)
        kv = tf(S)
        va = tf(QT, NG, 32)
        pt = [tf(R, S) for _ in range(2)]
        ot = tf(S)
        mx = tf(2, QT * R)
        rec = tf(QT * R)
        ks = tf(S)

        tr = carve(work_r[:, 13824 - 2 * KH * T:13824])
        on_hi, on_lo = tr(KH, T), tr(KH, T)
        on = xn

        tf = carve(work_f)
        fw = []
        for nf in (NF0, NF1):
            tiles = carve(work_r)(nf, WS + WT)
            fw.append((tiles[:, :, 0:WS], tiles[:, :, WS:WS + WT]))
        tr = carve(work_r[:, NF0 * (WS + WT):13824])
        h_hi, h_lo = tr(4, S), tr(4, S)
        sg, su, hh = tf(2, S), tf(2, S), tf(2, S)
        compared = [[work_f[:, a + i * n:a + (i + 1) * n] for i in range(2)]
                    for a, n in ((KH * S + QT * S + 4 * QT, QT * E0 * E0), (6192, TT * E1 * E1))]

        s_x, s_c = [sem(f"s_xin{b}") for b in range(B)], sem("s_c")
        s_lt, s_lx, s_zero, s_nm = (sem(n) for n in ("s_lt", "s_lx", "s_zero", "s_nm"))
        s_raw, s_split, s_wh = sem("s_raw"), sem("s_split"), sem("s_wh")
        s_dve, s_xb, s_ve, s_rt = sem("s_dve"), sem("s_xb"), sem("s_ve"), sem("s_rt")
        s_xn, s_xnT, s_xh, s_xl = sem("s_xn"), sem("s_xnT"), sem("s_xh"), sem("s_xl")
        s_lg, s_ex, s_exd = sem("s_lg"), sem("s_ex"), sem("s_exd")
        s_gw, s_gt, s_wt = sem("s_gw"), sem("s_gt"), sem("s_wt")
        s_lc, s_g0, s_g1 = sem("s_lc"), sem("s_g0"), sem("s_g1")
        a_pj, a_hi, a_lo, a_vt, a_vx = sem("a_pj"), sem("a_hi"), sem("a_lo"), sem("a_vt"), sem("a_vx")
        a_vh, a_vl, a_sc, a_m, a_n = sem("a_vh"), sem("a_vl"), sem("a_sc"), sem("a_m"), sem("a_n")
        a_e, a_r, a_p, a_pt, a_ph, a_pl = (sem(n) for n in ("a_e", "a_r", "a_p", "a_pt", "a_ph", "a_pl"))
        a_cx, a_ch, a_cl, a_o, a_y = (sem(n) for n in ("a_cx", "a_ch", "a_cl", "a_o", "a_y"))
        f_gu, f_s, f_p, f_h, f_hi, f_lo, f_dn, f_y = (
            [sem(f"{n}{i}") for i in range(2)] for n in ("f_gu", "f_s", "f_p", "f_h", "f_hi", "f_lo", "f_dn", "f_y"))
        s_out = sem("s_out")
        b_pj, b_kv, b_hi, b_lo, b_vt, b_va = (sem(n) for n in ("b_pj", "b_kv", "b_hi", "b_lo", "b_vt", "b_va"))
        b_sq, b_qs, b_sk, b_ks, b_sn, b_mx = (sem(n) for n in ("b_sq", "b_qs", "b_sk", "b_ks", "b_sn", "b_mx"))
        b_m1, b_m2, b_mt, b_qm, b_st, b_ex = (sem(n) for n in ("b_m1", "b_m2", "b_mt", "b_qm", "b_st", "b_ex"))
        b_km = sem("b_km")
        b_pv, b_ot, b_ox, b_rc, b_on, b_nt = (sem(n) for n in ("b_pv", "b_ot", "b_ox", "b_rc", "b_on", "b_nt"))
        b_nh, b_nl, b_o, b_y = (sem(n) for n in ("b_nh", "b_nl", "b_o", "b_y"))

        block = ctx.enter_context(nc.Block())

        SPLIT_A0 = 1
        SPLIT_F0 = SPLIT_A0
        SPLIT_A1 = SPLIT_F0 + G0 * NF0 + 1
        SPLIT_F1 = SPLIT_A1

        def xt_bank(layer, b, k):
            return 2 * k + b if layer == 1 and b < 2 else 2 * b + k

        def turns(s, following):
            if following and s == NG - 1:
                return {"maxima": 1, "project": 4, "stack_k": 7, "stack_q": 10, "outputs": 14}
            if s == NG + 1:
                return {"maxima": 1, "values": 4, "stack_k": 6, "stack_q": 9, "outputs": 14, "project": QT * R}
            if following and s in (NG - 3, NG - 2):
                return {"maxima": 1, "stack_k": 5, "stack_q": 9, "outputs": 11, "project": 13}
            return {"maxima": 1, "stack_k": 5, "stack_q": 9, "outputs": 14, "project": QT * R}

        @block.sync
        def _(sp):
            for b in range(B):
                sp.dma_start(x[:, b * QT:(b + 1) * QT, :],
                             x_in[b * S:(b + 1) * S, :].rearrange("(t p) h -> p t h", p=P)).then_inc(s_x[b], 16)
            sp.dma_start(const[:], const_in).then_inc(s_c, 16)
            sp.dma_start(bias[:], bias_in).then_inc(s_c, 16)
            sp.dma_start(raw[:, 0:AW0], aw0_in).then_inc(s_raw, 16)
            with sp.Fori(0, G0) as g:
                sp.wait_ge(s_split, g * NF0 + SPLIT_F0)
                sp.dma_start(raw[:], ffn0_in[bass.ts(g, P), :]).then_inc(s_raw, 16)
            sp.wait_ge(s_split, SPLIT_F0 + G0 * NF0)
            sp.dma_start(raw[:, 0:AW1], aw1_in).then_inc(s_raw, 16)
            sp.dma_start(raw[:, AW1:AW1 + NSELQ + NSELK], sel_in).then_inc(s_raw, 16)
            with sp.Fori(0, G1) as g:
                sp.wait_ge(s_split, g * NF1 + SPLIT_F1)
                sp.dma_start(raw[:, 0:NF1 * WS], ffn1_in[bass.ts(g, P), :]).then_inc(s_raw, 16)
            for b in range(B):
                sp.wait_ge(f_y[1], (G1 - 1) * B + b + 2)
                sp.dma_start(out[b * S:(b + 1) * S, :].rearrange("(t p) h -> p t h", p=P),
                             x[:, b * QT:(b + 1) * QT, :]).then_inc(s_out, 16)
            sp.wait_ge(s_out, 16 * B)

        @block.gpsimd
        def _(pool):
            nc.gpsimd.memset(zero[:, 0:1], 0.0).then_inc(s_zero, 1)
            nc.gpsimd.memset(zero[:, 1:2], -0.5).then_inc(s_zero, 1)
            pool.wait_ge(s_zero, 2)

            def high(o, i):
                return nc.gpsimd.tensor_tensor(o, i, zero[:, 0:1].broadcast_to([P, i.shape[1]]), ALU.add)

            def root(layer, b):
                pool.wait_ge(s_ve, layer * B + b + 1)
                nc.gpsimd.tensor_tensor(rs[:, 2, b * QT:(b + 1) * QT], rs[:, 0, b * QT:(b + 1) * QT],
                                        zero[:, 1:2].broadcast_to([P, QT]), ALU.pow).then_inc(s_rt, 1)

            for b in range(B):
                root(0, b)

            def add_bias(layer):
                pool.wait_ge(s_xn, (layer + 1) * TT)
                nc.gpsimd.tensor_tensor(x[:], x[:], bo[layer].unsqueeze(1).broadcast_to([P, TT, H]),
                                        ALU.add).then_inc(s_xb, 1)

            def split_tile(layer, f, wh):
                fw_hi, fw_lo = fw[layer]
                high(fw_hi[:, f, :], raw[:, f * WS:(f + 1) * WS]).then_inc(s_wh, 1)
                pool.wait_ge(s_wh, wh)
                nc.gpsimd.tensor_tensor(fw_lo[:, f, :], raw[:, f * WS:f * WS + WT],
                                        fw_hi[:, f, 0:WT].bitcast(f32), ALU.subtract).then_inc(s_split, 1)

            pool.wait_ge(s_c, 32)
            add_bias(0)
            pool.wait_ge(s_raw, 2 * 16)
            pool.wait_ge(a_sc, B * QT)
            for f in range(NF0):
                if (f + 1) * (WS + WT) > 4 * KH * S:
                    pool.wait_ge(a_cx, KH * B)
                split_tile(0, f, 1 + f + 1)
            for g in range(1, G0):
                pool.wait_ge(s_raw, g * 16 + 2 * 16)
                for f in range(NF0):
                    pool.wait_ge(f_dn[0], g * (B * NF0) + (f + 1 - NF0))
                    split_tile(0, f, g * NF0 + (1 + f + 1))
            pool.wait_ge(s_raw, (G0 + 3) * 16)
            high(awr[:, 0:AW1], raw[:, 0:AW1]).then_inc(s_wh, 1)
            pool.wait_ge(s_wh, 1 + G0 * NF0 + 1)
            high(awr[:, 2 * AW1:2 * AW1 + NSELQ + NSELK], raw[:, AW1:AW1 + NSELQ + NSELK])
            nc.gpsimd.tensor_tensor(awr[:, AW1:2 * AW1], raw[:, 0:AW1], awr[:, 0:AW1].bitcast(f32),
                                    ALU.subtract).then_inc(s_split, 1)
            for b in range(B):
                root(1, b)
            def key_copies(b, g):
                pool.wait_ge(b_ks, b * NG + (g + 1))
                for r in range(R):
                    ins = nc.gpsimd.tensor_tensor(km[g % 4][:, r, :], ks, head_rows[:, r:r + 1].broadcast_to([P, S]),
                                                  ALU.mult)
                ins.then_inc(b_km, 1)

            for g in range(NG):
                key_copies(0, g)
                if g == 1:
                    add_bias(1)
            with pool.Fori(1, B) as b:
                for g in range(NG):
                    key_copies(b, g)
            pool.wait_ge(s_raw, (G0 + 4) * 16)
            pool.wait_ge(b_st, 2 * B * NG * QT)
            pool.wait_ge(s_gw, B + 1)
            for f in range(NF1):
                if (f + 1) * (WS + WT) > 13824 - 2 * KH * T:
                    pool.wait_ge(b_o, B)
                split_tile(1, f, 2 + G0 * NF0 + f + 1)
            for g in range(1, G1):
                pool.wait_ge(s_raw, g * 16 + (G0 + 4) * 16)
                for f in range(NF1):
                    pool.wait_ge(f_dn[1], g * (B * NF1) + (f + 1 - NF1))
                    split_tile(1, f, g * NF1 + (2 + G0 * NF0 + f + 1))

        @block.tensor
        def _(pe):
            def mm3(o, w_hi, w_lo, x_hi, x_lo, first, last):
                nc.tensor.matmul(o, w_hi, x_hi, start=first, stop=False)
                nc.tensor.matmul(o, w_hi, x_lo, start=False, stop=False)
                return nc.tensor.matmul(o, w_lo, x_hi, start=False, stop=last)

            def tokens_t(layer, b):
                pe.wait_ge(s_xn, layer * TT + (b + 1) * QT)
                for k in range(KH):
                    for t in range(QT):
                        ins = nc.tensor.transpose(psum[:, xt_bank(layer, b, k), t * P:(t + 1) * P],
                                                  xn[:, b * QT + t, k * P:(k + 1) * P], ident)
                    ins.then_inc(s_xnT, 1)

            def logits(layer, b, o):
                gate_hi, gate_lo = (w0_hi[2], w0_lo[2]) if layer == 0 else (w1_hi[2], w1_lo[2])
                tok = slice(b * S, (b + 1) * S)
                for k in range(KH):
                    ins = mm3(o, gate_hi[k], gate_lo[k], xt_hi[:, k, tok], xt_lo[:, k, tok], k == 0, k == KH - 1)
                ins.then_inc(s_lg, 1)

            def logits_by_token(layer):
                for b in range(B):
                    pe.wait_ge(s_lt, layer * B + b + 1)
                    for t in range(QT):
                        ins = nc.tensor.transpose(psum[:, 4 + b, t * P:(t + 1) * P], lt[layer][:, b, t * P:(t + 1) * P],
                                                  ident)
                ins.then_inc(s_lx, 1)

            def to_tokens(bank, y_hi, y_lo, w_hi, w_lo, first, last):
                for t in range(QT):
                    tok = slice(t * P, (t + 1) * P)
                    ins = mm3(psum[:, bank + t // 2, (t % 2) * H:(t % 2 + 1) * H], y_hi[:, tok], y_lo[:, tok],
                              w_hi, w_lo, first and t % 2 == 0, last and t % 2 == 1)
                return ins

            def gating_transposes(layer, cols):
                pe.wait_ge(s_gw, B + layer)
                for t in range(TT):
                    ins = nc.tensor.transpose(psum[:, 4 - layer + t // 4, (t % 4) * P:(t % 4 + 1) * P],
                                              gw[:, t * cols:t * cols + P].bitcast(f32), ident)
                ins.then_inc(s_gt, 1)

            def feed_forward(layer, nf, groups, split0, free):
                gu, h, lo, dn, yf = (s[layer] for s in (f_gu, f_h, f_lo, f_dn, f_y))
                fw_hi, fw_lo = fw[layer]
                nt = B * nf
                rows = LN_COLS1 if layer else LN_COLS

                def up(j, g, g_off):
                    k, f = j // nf, j % nf
                    pe.wait_ge(s_split, g * nf + (split0 + f + 1 + g_off * nf))
                    if not (isinstance(g, int) and j < 2):
                        pe.wait_ge(h, g * nt + (j - 1 + g_off * nt))
                    tok = slice(k * S, (k + 1) * S)
                    for c in range(2):
                        for i in range(KH):
                            col = (c * KH + i) * P
                            mm3(psum[:, 2 * c + j % 2, :], fw_hi[:, f, col:col + P], fw_lo[:, f, col:col + P],
                                xt_hi[:, i, tok], xt_lo[:, i, tok], i == 0, i == KH - 1)
                    if isinstance(g, int) and j == 0:
                        pe.wait_ge(s_wt, layer + 1)
                        free()
                    nc.tensor.matmul(psum[:, 4 + j % 2, :], fw_hi[0:rows, f, WT:WS], wt[0:rows, tok],
                                     start=True, stop=True).then_inc(gu, 1)

                def down(j, g):
                    k, f = j // nf, j % nf
                    pe.wait_ge(lo, g * nt + (j + 1))
                    if f == 0:
                        pe.wait_ge(yf, g * B + (k + 1))
                    to_tokens(6, h_hi[:, j % 4, :], h_lo[:, j % 4, :], fw_hi[:, f, WC:WT], fw_lo[:, f, WC:WT],
                              f == 0, f == nf - 1).then_inc(dn, 1)

                up(0, 0, 0)
                up(1, 0, 0)
                with pe.Fori(0, groups - 1) as g:
                    for j in range(nt):
                        if j + 2 < nt:
                            up(j + 2, g, 0)
                        else:
                            up(j + 2 - nt, g, 1)
                        down(j, g)
                for j in range(nt):
                    if j + 2 < nt:
                        up(j + 2, groups - 1, 0)
                    if j == nt - 1 and layer == 0:
                        tokens_t(1, 0)
                    down(j, groups - 1)

            pe.wait_ge(s_c, 32)
            for b in range(B - 1):
                tokens_t(0, b)

            def project0(n0, n1, b1, o0):
                for n in range(n0, n1):
                    for i in range(KH):
                        ins = mm3(psum[:, o0 + n - n0, :], w0_hi[0][:, i, n * P:(n + 1) * P], w0_lo[0][:, i, n * P:(n + 1) * P],
                                  xt_hi[:, i, bass.ts(b1, S)], xt_lo[:, i, bass.ts(b1, S)], i == 0, i == KH - 1)
                    ins.then_inc(a_pj, 1)

            def values_by_key0(b1):
                for t in range(QT):
                    for c in range(KH):
                        ins = nc.tensor.transpose(psum[:, 6 + t // 2, (t % 2) * H + c * P:(t % 2) * H + (c + 1) * P],
                                                  vt[:, c, t * P:(t + 1) * P], ident)
                    if t % 2:
                        ins.then_inc(a_vx, 1)

            def attention0(b, last):
                pe.wait_ge(a_lo, b * 4 + 4)
                for t in range(QT):
                    if t == 2:
                        pe.wait_ge(a_y, b + 1)
                    for i in range(KH):
                        q = slice(t * P, (t + 1) * P)
                        ins = mm3(psum[:, t, :], qk_hi[:, i, q], qk_lo[:, i, q], qk_hi[:, 2 + i, :],
                                  qk_lo[:, 2 + i, :], i == 0, i == KH - 1)
                    ins.then_inc(a_sc, 1)
                pe.wait_ge(a_vl, b * 2 + 2)
                if not last:
                    project0(0, 4, b + 1, 4)
                for t in range(QT):
                    pe.wait_ge(a_p, b * QT + (t + 1))
                    if not last:
                        pe.wait_ge(a_lo, b * 4 + (5 + t))
                    for c in range(QT):
                        ins = nc.tensor.transpose(psum[:, 4 + t, c * P:(c + 1) * P], prob[:, t, c * P:(c + 1) * P], ident)
                    ins.then_inc(a_pt, 1)
                if not last:
                    project0(4, 6, b + 1, 2)
                pe.wait_ge(a_pl, b * QT + QT)
                for c in range(KH):
                    for t in range(QT):
                        ins = mm3(psum[:, c, :], v_hi[:, t, c * P:(c + 1) * P], v_lo[:, t, c * P:(c + 1) * P],
                                  p_hi[:, t, :], p_lo[:, t, :], t == 0, t == QT - 1)
                    ins.then_inc(a_cx, 1)
                if not last:
                    pe.wait_ge(a_vt, b * 2 + 4)
                    values_by_key0(b + 1)
                pe.wait_ge(a_cl, b * 2 + 2)
                for i in range(KH):
                    ins = to_tokens(2, c_hi[:, i, :], c_lo[:, i, :], w0_hi[1][:, i, :], w0_lo[1][:, i, :],
                                    i == 0, i == KH - 1)
                ins.then_inc(a_o, 1)

            pe.wait_ge(s_split, SPLIT_A0)
            pe.wait_ge(s_xl, 4)
            project0(0, 4, 0, 0)
            tokens_t(0, B - 1)
            for b in range(B):
                if b % 2 == 0:
                    pe.wait_ge(s_xl, 6 + b)
                logits(0, b, psum[:, 4 + b, :])
            logits_by_token(0)
            pe.wait_ge(s_lc, 1)
            project0(4, 6, 0, 4)
            pe.wait_ge(a_vt, 2)
            values_by_key0(0)
            pe.wait_ge(a_lo, 4)
            with pe.Fori(0, B - 1) as b:
                attention0(b, False)
            attention0(B - 1, True)
            gating_transposes(0, LN_COLS)
            pe.wait_ge(a_y, B + 1)
            feed_forward(0, NF0, G0, SPLIT_F0, lambda: None)
            NP, NQ = NG * QT * R, NG * QT

            def project(n, b1, o):
                for i in range(KH):
                    ins = mm3(o, w1_hi[0][:, i, n * P:(n + 1) * P], w1_lo[0][:, i, n * P:(n + 1) * P],
                              xt_hi[:, i, bass.ts(b1, S)], xt_lo[:, i, bass.ts(b1, S)], i == 0, i == KH - 1)
                ins.then_inc(b_pj, 1)

            def values_by_key(o):
                for t in range(QT):
                    ins = nc.tensor.transpose(o[:, t * P:(t + 1) * P], kv[:, t * P:(t + 1) * P], ident)
                ins.then_inc(b_vt, 1)

            def stack_q(g):
                nc.tensor.matmul(psum[:, 0, :], selq[:, 0, g % 4, :], qc_hi[:, g % NG // 4, :], start=True, stop=False)
                nc.tensor.matmul(psum[:, 0, :], selq[:, 1, g % 4, :], qc_lo[:, g % NG // 4, :],
                                 start=False, stop=True).then_inc(b_sq, 1)

            def stack_k(g):
                nc.tensor.matmul(psum[:, 0, :], selk[0:64, 0, g % NG, :], kc_hi[0:64, :], start=True, stop=False)
                nc.tensor.matmul(psum[:, 0, :], selk[0:64, 1, g % NG, :], kc_lo[0:64, :],
                                 start=False, stop=True).then_inc(b_sk, 1)

            def scores(b, g, i):
                if not (isinstance(b, int) and b * NG + g == 0 and i < 2):
                    pe.wait_ge(b_mx, b * NP + (g * QT * R + i - 1))
                t, r = i // R, i % R
                nc.tensor.matmul(psum[:, 1 + i % 2, :], qs[g % 2][:, t * P:(t + 1) * P],
                                 km[g % 4][:, r, :], start=True, stop=True).then_inc(b_sn, 1)

            def scores_t(b, g, i):
                t, h = i // 2, i % 2
                if g >= 1 or i >= 2:
                    pe.wait_ge(b_ex, b * (2 * NQ) + (g * 2 * QT + i - 1))
                for r in (2 * h, 2 * h + 1):
                    ins = nc.tensor.matmul(psum[:, 3 + 2 * h + r % 2, :], km[g % 4][:, r, t * P:(t + 1) * P],
                                           qm[g % 2], start=True, stop=True)
                ins.then_inc(b_st, 1)

            def values(b, g, t):
                pe.wait_ge(b_ex, b * (2 * NQ) + ((g * QT + t) * 2 + 2))
                if t == 0 and g >= 1:
                    pe.wait_ge(b_ot, b * NG + g)
                if t == 0 and g % NG == 0:
                    pe.wait_ge(b_va, b + (g // NG + 1))
                for r in range(R):
                    ins = nc.tensor.matmul(psum[32 * r:32 * r + 32, 7, :], va[:, t, g % NG, :], pt[t % 2][:, r, :],
                                           start=(t == 0), stop=(t == QT - 1), tile_position=(0, 32 * r))
                ins.then_inc(b_pv, 1)

            def outputs_t(b, g):
                pe.wait_ge(b_ot, b * NG + (g + 1))
                for t in range(QT):
                    ins = nc.tensor.transpose(psum[:, 0, t * P:(t + 1) * P], ot[:, t * P:(t + 1) * P], ident)
                ins.then_inc(b_ox, 1)

            def maxima_t(b, g):
                pe.wait_ge(b_m2, b * NG + (g + 1))
                for t in range(QT):
                    ins = nc.tensor.transpose(psum[:, 0, t * P:(t + 1) * P],
                                              mz[:, t].rearrange("p r c -> p (r c)").bitcast(f32), ident)
                ins.then_inc(b_mt, 1)

            TRANSPOSED = (3, 4, 6, 7, 10, 11, 13, 15)
            VALUED = (8, 12)

            def stage(b, s, last):
                front, back, stacks = not (last and s == NG), s >= 1, not (last and s >= NG - 1)
                following = not last and s >= 1
                turn = turns(s, following)
                for i in range(QT * R):
                    if i == 0:
                        if front:
                            pe.wait_ge(b_km, b * NG + (s + 1))
                    if front:
                        scores(b, s, i)
                    if i in (0, 2) and s >= 2:
                        values(b, s - 2, QT - 2 + i // 2)
                    if i == turn["maxima"] and back:
                        if s == 2:
                            pe.wait_ge(b_on, b * NG + 1)
                        if s <= 2:
                            pe.wait_ge(b_qs, b * NG + (s + 1))
                        elif not last and s in (NG - 2, NG - 1):
                            pe.wait_ge(b_lo, b * 3 + (s - (NG - 2) + 4))
                        else:
                            pe.wait_ge(b_on, b * NG + (s - 1))
                        maxima_t(b, s - 1)
                    if i == TRANSPOSED[0] and back:
                        pe.wait_ge(b_qm, b * NG + s)
                    if back:
                        if i in TRANSPOSED:
                            scores_t(b, s - 1, TRANSPOSED.index(i))
                        if i in VALUED:
                            values(b, s - 1, VALUED.index(i))
                    projects = following and NG - 3 <= s < NG
                    if i == turn["project"] and projects:
                        if s < NG - 1:
                            pe.wait_ge(b_on, b * NG + s)
                        project(s - (NG - 3), b + 1, psum[:, 0, :])
                    if s == NG + 1 and i == turn["values"]:
                        values_by_key(psum[:, 0, :])
                    if i == turn["stack_k"] and stacks:
                        if projects and s == NG - 1:
                            pe.wait_ge(b_hi, b * 3 + 6)
                            pe.wait_ge(b_lo, b * 3 + 6)
                        if s == NG + 1:
                            pe.wait_ge(b_va, b + 2)
                        stack_k(s + 1)
                    if i == turn["stack_q"] and stacks:
                        pe.wait_ge(b_ks, b * NG + (s + 2))
                        stack_q(s + 1)
                    if i == turn["outputs"] and s >= 2:
                        if stacks:
                            pe.wait_ge(b_qs, b * NG + (s + 2))
                        outputs_t(b, s - 2)
                    if s == 0 and i in (3, 6, 9, 12):
                        n = (3, 6, 9, 12).index(i)
                        pe.wait_ge(s_xl, 2 * B + (6 if n < 2 else 8))
                        logits(1, n, psum[:, 4 + n, :])
                if not front:
                    values(b, s - 1, QT - 2)
                    values(b, s - 1, QT - 1)

            def sequence(b, last):
                for s in range(2, NG + (1 if last else 2)):
                    stage(b, s, last)
                if last:
                    gating_transposes(1, LN_COLS1)
                    pe.wait_ge(b_on, b * NG + NG)
                    outputs_t(b, NG - 1)

            tokens_t(1, 1)
            tokens_t(1, 2)
            pe.wait_ge(s_split, SPLIT_A1)
            pe.wait_ge(s_xl, 2 * B + 2)
            project(2, 0, psum[:, 0, :])
            project(0, 0, psum[:, 2, :])
            pe.wait_ge(s_xl, 2 * B + 4)
            project(1, 0, psum[:, 1, :])
            pe.wait_ge(b_lo, 1)
            stack_k(0)
            pe.wait_ge(b_kv, 1)
            values_by_key(psum[:, 3, :])
            pe.wait_ge(b_ks, 1)
            pe.wait_ge(b_lo, 3)
            stack_q(0)
            tokens_t(1, B - 1)
            pe.wait_ge(b_qs, 1)
            stage(0, 0, False)
            logits_by_token(1)
            pe.wait_ge(s_lc, 2)
            stage(0, 1, False)
            with pe.Fori(0, B - 1) as b:
                sequence(b, False)
            sequence(B - 1, True)
            pe.wait_ge(b_on, B * NG + 1)
            for b in range(B):
                if b == 1:
                    pe.wait_ge(s_wt, 2)
                for k in range(KH):
                    for t in range(QT):
                        ins = nc.tensor.transpose(psum[:, 2 * b + k, t * P:(t + 1) * P],
                                                  on[:, b * QT + t, k * P:(k + 1) * P], ident)
                    ins.then_inc(b_nt, 1)
            for b in range(B):
                tok = slice(b * S, (b + 1) * S)
                pe.wait_ge(b_nl, 2 * b + 2)
                for i in range(KH):
                    ins = to_tokens(2 * b, on_hi[:, i, tok], on_lo[:, i, tok], w1_hi[1][:, i, :], w1_lo[1][:, i, :],
                                    i == 0, i == KH - 1)
                ins.then_inc(b_o, 1)
            pe.wait_ge(b_y, 2)
            feed_forward(1, NF1, G1, SPLIT_F1, lambda: pe.wait_ge(b_y, B))

        @block.scalar
        def _(act):
            def copy(o, i):
                return nc.scalar.copy(o, i)

            def high_parts(layer, b):
                for k in range(KH):
                    act.wait_ge(s_xnT, layer * 2 * B + b * KH + k + 1)
                    copy(xt_hi[:, k, b * S:(b + 1) * S], psum[:, xt_bank(layer, b, k), :]).then_inc(s_xh, 1)

            def normalised(layer, b):
                act.wait_ge(s_nm, layer * B + b + 1)
                for t in range(b * QT, (b + 1) * QT):
                    nc.scalar.activation(xn[:, t, :], x[:, t, :], ACT.Identity, scale=rs[:, 4, t:t + 1],
                                         bias=rs[:, 7, t:t + 1]).then_inc(s_xn, 1)

            def logits(layer, b, o):
                act.wait_ge(s_lg, layer * B + b + 1)
                copy(lt[layer][:, b, :], o).then_inc(s_lt, 1)

            def gating_exp(ne, count, n):
                act.wait_ge(s_ex, count)
                nc.scalar.activation(pr[:, 0:n, 0:ne], pr[:, 0:n, 0:ne], ACT.Exp).then_inc(s_exd, 1)

            def gating_weights(layer):
                act.wait_ge(s_gt, layer + 1)
                rows = LN_COLS1 if layer else LN_COLS
                copy(wt[0:rows, :].rearrange("p (a b) -> p a b", a=B), psum[0:rows, 4 - layer:8 - layer, :]).then_inc(s_wt, 1)

            def feed_forward(layer, nf, groups):
                gu, s, h, hi = (q[layer] for q in (f_gu, f_s, f_h, f_hi))
                nt = B * nf

                def group(g, norms):
                    for j in range(nt):
                        act.wait_ge(gu, g * nt + (j + 1))
                        nc.scalar.activation(sg[:, j % 2, :], psum[:, j % 2, :], ACT.Silu).then_inc(s, 1)
                        act.wait_ge(h, g * nt + (j + 1))
                        copy(h_hi[:, j % 4, :], hh[:, j % 2, :]).then_inc(hi, 1)
                        if norms and nf < j < nt - nf and j % nf == 3:
                            normalised(1, j // nf - 1)

                with act.Fori(0, groups - 1) as g:
                    group(g, False)
                group(groups - 1, layer == 0)

            for b in range(B):
                normalised(0, b)
                if b >= 1:
                    high_parts(0, b - 1)
                if b == 2:
                    act.wait_ge(s_raw, 16)
                    copy(awr[:, 0:AW0], raw[:, 0:AW0]).then_inc(s_wh, 1)

            def projections(b1, o0):
                for n in range(4):
                    act.wait_ge(a_pj, b1 * 6 + (n + 1))
                    nc.scalar.activation(qk_hi[:, n, :], psum[:, o0 + n, :], ACT.Identity, bias=bq0[:, n:n + 1]).then_inc(a_hi, 1)

            def values_projected(b1, o0):
                for n in (4, 5):
                    act.wait_ge(a_pj, b1 * 6 + (n + 1))
                    nc.scalar.activation(vt[:, n - 4, :], psum[:, o0 + n - 4, :], ACT.Identity, bias=bq0[:, n:n + 1]).then_inc(a_vt, 1)

            def values_by_key0(b1):
                for c in range(2):
                    act.wait_ge(a_vx, b1 * 2 + (c + 1))
                    copy(v_hi[:, 2 * c:2 * c + 2, :], psum[:, 6 + c, :].rearrange("p (t h) -> p t h", h=H)).then_inc(a_vh, 1)

            def attention0(b, last):
                for t in range(QT):
                    act.wait_ge(a_n, b * QT + (t + 1))
                    nc.scalar.activation(prob[:, t, :], psum[:, t, :], ACT.Exp, scale=1.0 / 16.0, bias=sm[:, 1, t:t + 1],
                                         accum_out=sm[:, 2, t:t + 1]).then_inc(a_e, 1)
                if not last:
                    projections(b + 1, 4)
                for t in range(QT):
                    act.wait_ge(a_pt, b * QT + (t + 1))
                    copy(p_hi[:, :, t * P:(t + 1) * P], psum[:, 4 + t, :].rearrange("p (c q) -> p c q", q=P)).then_inc(a_ph, 1)
                gating_exp(E0, b + 1, QT)
                if not last:
                    values_projected(b + 1, 2)
                for c in range(KH):
                    act.wait_ge(a_cx, b * 2 + (c + 1))
                    copy(c_hi[:, c, :], psum[:, c, :]).then_inc(a_ch, 1)
                if not last:
                    values_by_key0(b + 1)

            act.wait_ge(s_c, 32)
            projections(0, 0)
            high_parts(0, B - 1)
            for b in range(B):
                logits(0, b, psum[:, 4 + b, :])
            values_projected(0, 4)
            values_by_key0(0)
            with act.Fori(0, B - 1) as b:
                attention0(b, False)
            attention0(B - 1, True)
            gating_weights(0)
            feed_forward(0, NF0, G0)
            def compact(n, b1, o, at=None):
                act.wait_ge(b_pj, b1 * 3 + ((n if at is None else at) + 1))
                if n < 2:
                    nc.scalar.activation(qc_hi[:, n, :], o, ACT.Identity, bias=bq1[:, n:n + 1]).then_inc(b_hi, 1)
                else:
                    nc.scalar.activation(kv[:], o, ACT.Identity, bias=bq1[:, 2:3]).then_inc(b_kv, 1)
                    nc.scalar.activation(kc_hi[:], o, ACT.Identity, bias=bq1[:, 2:3]).then_inc(b_hi, 1)

            def stack_q(b, g):
                act.wait_ge(b_sq, b * NG + (g + 1))
                copy(qs[g % 2], psum[:, 0, :]).then_inc(b_qs, 1)

            def stack_k(b, g):
                act.wait_ge(b_sk, b * NG + (g + 1))
                if g >= 1:
                    act.wait_ge(b_km, b * NG + g)
                nc.scalar.activation(ks, psum[:, 0, :], ACT.Identity, bias=kone).then_inc(b_ks, 1)

            def outputs(b, g):
                act.wait_ge(b_pv, b * (NG * QT) + (g + 1) * QT)
                if g >= 1:
                    act.wait_ge(b_ox, b * NG + g)
                copy(ot[:], psum[:, 7, :]).then_inc(b_ot, 1)

            def stage(b, s, last):
                back, stacks = s >= 1, not (last and s >= NG - 1)
                following = not last and s >= 1
                if s >= 2:
                    outputs(b, s - 2)
                if last and s == NG:
                    gating_exp(E1, B + 1, TT)
                for t in range(QT):
                    if back:
                        g = s - 1
                        for h in range(2):
                            act.wait_ge(b_st, b * (2 * NG * QT) + ((g * QT + t) * 2 + h + 1))
                            if g * QT + t >= 2:
                                act.wait_ge(b_pv, b * (NG * QT) + (g * QT + t - 1))
                            nc.scalar.activation(pt[t % 2][:, 2 * h:2 * h + 2, :], psum[:, 3 + 2 * h:5 + 2 * h, :],
                                                 ACT.Exp, scale=float(HD) ** -0.5).then_inc(b_ex, 1)
                    if following and s == NG - 1:
                        if t == 0:
                            compact(2, b + 1, psum[:, 0, :])
                        if t == 1:
                            stack_k(b, s + 1)
                        if t == 2:
                            stack_q(b, s + 1)
                    elif stacks:
                        if t == 0:
                            stack_k(b, s + 1)
                        if t == 1:
                            stack_q(b, s + 1)
                        if t == 2 and following and s in (NG - 3, NG - 2):
                            compact(s - (NG - 3), b + 1, psum[:, 0, :])
                if last and s == NG:
                    outputs(b, s - 1)

            high_parts(1, 0)
            normalised(1, B - 2)
            high_parts(1, 1)
            compact(2, 0, psum[:, 0, :], 0)
            compact(0, 0, psum[:, 2, :], 1)
            high_parts(1, 2)
            normalised(1, B - 1)
            stack_k(0, 0)
            compact(1, 0, psum[:, 1, :], 2)
            stack_q(0, 0)
            high_parts(1, 3)
            logits(1, 0, psum[:, 4, :])
            stack_k(0, 1)
            logits(1, 1, psum[:, 5, :])
            stack_q(0, 1)
            for b in range(2, B):
                logits(1, b, psum[:, 4 + b, :])
            stage(0, 1, False)
            with act.Fori(0, B - 1) as b:
                for s in range(2, NG + 2):
                    stage(b, s, False)
            for s in range(2, NG + 1):
                stage(B - 1, s, True)
            gating_weights(1)
            for n in range(2 * B):
                act.wait_ge(b_nt, n + 1)
                b, k = n // KH, n % KH
                copy(on_hi[:, k, b * S:(b + 1) * S], psum[:, n, :]).then_inc(b_nh, 1)
            feed_forward(1, NF1, G1)

        @block.vector
        def _(dve):
            v = nc.vector
            done = [0]

            def then(ins):
                done[0] += 1
                ins.then_inc(s_dve, 1)
                dve.wait_ge(s_dve, done[0])

            def moments(layer, b):
                for t in range(b * QT, (b + 1) * QT):
                    ins = v.bn_stats(st[:, t, :], x[:, t, :])
                then(ins)
                for t in range(b * QT, (b + 1) * QT):
                    ins = v.bn_aggr(mv[:, t, :], st[:, t, :])
                then(ins)
                tiles = slice(b * QT, (b + 1) * QT)
                v.tensor_scalar(rs[:, 0, tiles], mv[:, tiles, 1], EPS, None, ALU.add).then_inc(s_ve, 1)

            def root(layer, b):
                tiles = slice(b * QT, (b + 1) * QT)
                ve, r0, t1, rstd = (rs[:, i, tiles] for i in (0, 2, 3, 4))
                dve.wait_ge(s_rt, layer * B + b + 1)
                then(v.tensor_tensor(t1, r0, r0, ALU.mult))
                then(v.tensor_tensor(t1, t1, ve, ALU.mult))
                then(v.tensor_scalar(t1, t1, -0.5, 1.5, ALU.mult, ALU.add))
                then(v.tensor_tensor(rstd, r0, t1, ALU.mult))
                v.scalar_tensor_tensor(out=rs[:, 7, tiles], in0=mv[:, tiles, 0], scalar=-1.0, in1=rstd,
                                       op0=ALU.mult, op1=ALU.mult).then_inc(s_nm, 1)

            def low_parts(layer, b):
                for k in range(KH):
                    dve.wait_ge(s_xh, layer * 2 * B + b * KH + k + 1)
                    tok = slice(b * S, (b + 1) * S)
                    v.tensor_tensor(xt_lo[:, k, tok], psum[:, xt_bank(layer, b, k), :], xt_hi[:, k, tok].bitcast(f32),
                                    ALU.subtract).then_inc(s_xl, 1)

            def take_logits(layer, ne):
                ne1 = ne + 1
                then(v.memset(gw[:].bitcast(mybir.dt.uint32), 0))
                then(v.memset(gw[:, 0:TT * 2 * ne1].rearrange("p (t c) -> p t c", c=2 * ne1)[:, :, ne:ne1].bitcast(f32),
                              1.0))
                dve.wait_ge(s_lx, layer + 1)
                logits = psum[:, 4:8, :].rearrange("p b (t e) -> p (b t) e", e=P)[:, :, 0:ne]
                if layer == 0:
                    v.tensor_copy(lg[:, :, 0:ne], logits).then_inc(s_lc, 1)
                else:
                    v.tensor_tensor(lg[:, :, 0:ne], logits, gate_b.unsqueeze(1).broadcast_to([P, TT, ne]),
                                    ALU.add).then_inc(s_lc, 1)
                dve.wait_ge(s_lc, layer + 1)

            def gating(layer, ne, top, count, tiles, n, chain, base):
                step = [0]
                assert layer == 1 or n == QT

                def then(ins):
                    step[0] += 1
                    ins.then_inc(chain, 1)
                    dve.wait_ge(chain, base + step[0])

                ne1 = ne + 1
                l, p, rk = lg[:, tiles, 0:ne], pr[:, 0:n, 0:ne], rank[:, 0:n, 0:ne]
                if layer == 0:
                    l = rank[:, QT:2 * QT, 0:ne]
                sm5, sm6, sm7 = (rs[:, i, 0:n] for i in (5, 6, 7))
                col = lambda c: c.unsqueeze(2).broadcast_to([P, n, ne])

                def exponents():
                    if layer == 0:
                        then(v.tensor_copy(l, lg[:, tiles, 0:ne]))
                    then(v.reduce_max(sm5, l, AX.X))
                    v.tensor_tensor(p, l, col(sm5), ALU.subtract).then_inc(s_ex, 1)

                def comparisons():
                    dve.wait_ge(s_exd, count)
                    then(v.reduce_sum(sm6, p, AX.X))
                    then(v.reciprocal(sm7, sm6))
                    then(v.tensor_tensor(p, p, col(sm7), ALU.mult))
                    ca, cb = (c[:, 0:n * ne * ne].rearrange("p (t a b) -> p t a b", a=ne, b=ne) for c in compared[layer])
                    if layer == 1:
                        then(v.tensor_tensor(l, p, route_b.unsqueeze(1).broadcast_to([P, n, ne]), ALU.add))
                    low = (low0, low1)[layer].rearrange("p (a b) -> p a b", b=ne).unsqueeze(1).broadcast_to([P, n, ne, ne])
                    other = l.unsqueeze(2).broadcast_to([P, n, ne, ne])
                    own = l.unsqueeze(3).broadcast_to([P, n, ne, ne])
                    v.tensor_tensor(ca, other, own, ALU.is_gt)
                    then(v.tensor_tensor(cb, other, own, ALU.is_equal))
                    then(v.tensor_tensor(cb, cb, low, ALU.mult))
                    then(v.tensor_tensor(ca, ca, cb, ALU.add))

                def weights():
                    ca = compared[layer][0][:, 0:n * ne * ne].rearrange("p (t a b) -> p t a b", a=ne, b=ne)
                    then(v.tensor_reduce(rk, ca, AX.X, ALU.add))
                    then(v.tensor_scalar(rk, rk, float(top), None, ALU.is_lt))
                    then(v.tensor_tensor(p, p, rk, ALU.mult))
                    if layer == 1:
                        then(v.reduce_sum(sm6, p, AX.X))
                        then(v.reciprocal(sm7, sm6))
                        then(v.tensor_tensor(p, p, col(sm7), ALU.mult))
                    g = gw[:, 0:TT * 2 * ne1].rearrange("p (t c) -> p t c", c=2 * ne1)[:, tiles, :]
                    then(v.tensor_scalar(g[:, :, 0:ne], p, 1.0, None, ALU.mult))
                    v.tensor_tensor(g[:, :, ne1:ne1 + ne], p, g[:, :, 0:ne].bitcast(f32), ALU.subtract).then_inc(s_gw, 1)
                    return step[0]

                return exponents, comparisons, weights

            def add_to_tokens(tiles, bank):
                return v.tensor_tensor(x[:, tiles, :], x[:, tiles, :],
                                       psum[:, bank:bank + 2, :].rearrange("p c (t h) -> p (c t) h", h=H), ALU.add)

            def feed_forward(layer, nf, groups):
                gu, s, sp_, h, hi, lo, dn, yf = (q[layer] for q in (f_gu, f_s, f_p, f_h, f_hi, f_lo, f_dn, f_y))
                nt = B * nf
                v.memset(rs[:, 7, 0:1], 0.0).then_inc(yf, 1)

                def add_outputs(g, k):
                    dve.wait_ge(dn, g * nt + (k + 1) * nf)
                    add_to_tokens(slice(k % B * QT, (k % B + 1) * QT), 6).then_inc(yf, 1)

                def group(g, first, norms):
                    for j in range(nt):
                        dve.wait_ge(s, g * nt + (j + 1))
                        v.tensor_tensor(su[:, j % 2, :], sg[:, j % 2, :], psum[:, 2 + j % 2, :], ALU.mult).then_inc(sp_, 1)
                        dve.wait_ge(sp_, g * nt + (j + 1))
                        v.tensor_tensor(hh[:, j % 2, :], su[:, j % 2, :], psum[:, 4 + j % 2, :], ALU.mult).then_inc(h, 1)
                        if j % nf == 1 and (j > nf or not first):
                            add_outputs(g, j // nf - 1)
                        dve.wait_ge(hi, g * nt + (j + 1))
                        v.tensor_tensor(h_lo[:, j % 4, :], hh[:, j % 2, :], h_hi[:, j % 4, :].bitcast(f32),
                                        ALU.subtract).then_inc(lo, 1)
                        if norms and j > nf and j % nf == 2:
                            moments(1, j // nf - 1)
                            root(1, j // nf - 1)

                group(0, True, False)
                with dve.Fori(1, groups - 1) as g:
                    group(g, False, False)
                group(groups - 1, False, layer == 0)
                if layer == 0:
                    low_parts(1, 0)
                add_outputs(groups - 1, B - 1)
                if layer == 0:
                    dve.wait_ge(yf, groups * B + 1)
                    moments(1, B - 1)
                    low_parts(1, 1)
                    root(1, B - 1)

            def projections(b1, o0):
                for n in range(4):
                    dve.wait_ge(a_hi, b1 * 4 + (n + 1))
                    v.scalar_tensor_tensor(out=qk_lo[:, n, :], in0=psum[:, o0 + n, :], scalar=bq0[:, n:n + 1],
                                           in1=qk_hi[:, n, :].bitcast(f32), op0=ALU.add, op1=ALU.subtract).then_inc(a_lo, 1)

            for b in range(B):
                dve.wait_ge(s_x[b], 16)
                moments(0, b)
                if b >= 1:
                    root(0, b - 1)
            low_parts(0, 0)
            root(0, B - 1)
            low_parts(0, 1)
            dve.wait_ge(s_wh, 1)
            v.tensor_tensor(awr[:, AW0:2 * AW0], raw[:, 0:AW0], awr[:, 0:AW0].bitcast(f32),
                            ALU.subtract).then_inc(s_split, 1)
            low_parts(0, 2)
            dve.wait_ge(s_c, 32)
            projections(0, 0)
            low_parts(0, B - 1)
            take_logits(0, E0)

            def values_by_key0(b1):
                for c in range(2):
                    dve.wait_ge(a_vh, b1 * 2 + (c + 1))
                    v.tensor_tensor(v_lo[:, 2 * c:2 * c + 2, :], psum[:, 6 + c, :].rearrange("p (t h) -> p t h", h=H),
                                    v_hi[:, 2 * c:2 * c + 2, :].bitcast(f32), ALU.subtract).then_inc(a_vl, 1)

            def attention0(b, last):
                for t in range(QT):
                    dve.wait_ge(a_sc, b * QT + (t + 1))
                    v.reduce_max(sm[:, 0, t:t + 1], psum[:, t, :], AX.X).then_inc(a_m, 1)
                    dve.wait_ge(a_m, b * QT + (t + 1))
                    v.tensor_scalar(sm[:, 1, t:t + 1], sm[:, 0, t:t + 1], -1.0 / 16.0, None, ALU.mult).then_inc(a_n, 1)
                for t in range(QT):
                    dve.wait_ge(a_e, b * QT + (t + 1))
                    v.reciprocal(sm[:, 3, t:t + 1], sm[:, 2, t:t + 1]).then_inc(a_r, 1)
                    dve.wait_ge(a_r, b * QT + (t + 1))
                    v.tensor_scalar(prob[:, t, :], prob[:, t, :], sm[:, 3, t:t + 1], None, ALU.mult).then_inc(a_p, 1)
                if not last:
                    projections(b + 1, 4)
                exponents, comparisons, weights = gating(0, E0, TOP0, b + 1, bass.ts(b, QT), QT, s_g0, b * GATE_STEPS)
                exponents()
                for t in range(QT):
                    dve.wait_ge(a_ph, b * QT + (t + 1))
                    q = slice(t * P, (t + 1) * P)
                    v.tensor_tensor(p_lo[:, :, q], psum[:, 4 + t, :].rearrange("p (c q) -> p c q", q=P),
                                    p_hi[:, :, q].bitcast(f32), ALU.subtract).then_inc(a_pl, 1)
                comparisons()
                for c in range(KH):
                    dve.wait_ge(a_ch, b * 2 + (c + 1))
                    v.tensor_tensor(c_lo[:, c, :], psum[:, c, :], c_hi[:, c, :].bitcast(f32), ALU.subtract).then_inc(a_cl, 1)
                if not last:
                    values_by_key0(b + 1)
                steps = weights()
                assert steps == GATE_STEPS, steps
                dve.wait_ge(a_o, b + 1)
                add_to_tokens(bass.ts(b, QT), 2).then_inc(a_y, 1)

            v.memset(sm[:, 3, 0:1], 0.0).then_inc(a_y, 1)
            values_by_key0(0)
            dve.wait_ge(s_xb, 1)
            with dve.Fori(0, B - 1) as b:
                attention0(b, False)
            attention0(B - 1, True)
            feed_forward(0, NF0, G0)
            def clear():
                then(v.memset(va[:], 0.0))
                v.memset(va[:, :, :, HD:HD + 1], 1.0)
                then(v.memset(mz[:].bitcast(mybir.dt.uint32), 0))

            NP = NG * QT * R

            def compact(n, b1, o, at=None):
                dve.wait_ge(b_hi, b1 * 3 + ((n if at is None else at) + 1))
                if n < 2:
                    v.scalar_tensor_tensor(out=qc_lo[:, n, :], in0=o, scalar=bq1[:, n:n + 1],
                                           in1=qc_hi[:, n, :].bitcast(f32), op0=ALU.add, op1=ALU.subtract).then_inc(b_lo, 1)
                else:
                    v.tensor_tensor(kc_lo[:], kv[:], kc_hi[:].bitcast(f32), ALU.subtract).then_inc(b_lo, 1)

            def values_by_key(b1, o):
                dve.wait_ge(b_vt, b1 + 1)
                v.tensor_copy(va[:, :, :, 0:HD], o.rearrange("p (t c) -> p t c", c=P)[:, :, 64:128]
                              .rearrange("p t (g d) -> p t g d", d=HD)).then_inc(b_va, 1)

            def normalise(b, g):
                dve.wait_ge(b_ox, b * NG + (g + 1))
                o = psum[:, 0, :].rearrange("p (q c) -> p q c", c=32)
                v.reciprocal(rec[:].unsqueeze(2), o[:, :, HD:HD + 1]).then_inc(b_rc, 1)
                dve.wait_ge(b_rc, b * NG + (g + 1))
                v.tensor_tensor(on[:, bass.ts(b, QT), g * 32:(g + 1) * 32].rearrange("p t (r d) -> p t r d", d=HD),
                                o[:, :, 0:HD].rearrange("p (t r) d -> p t r d", r=R),
                                rec[:].rearrange("p (t r) -> p t r", r=R).unsqueeze(3).broadcast_to([P, QT, R, HD]),
                                ALU.mult).then_inc(b_on, 1)

            def stage(b, s, last):
                front, following = not (last and s == NG), not last and s >= 1
                if not front:
                    exponents, comparisons, weights = gating(1, E1, TOP1, B + 1, slice(0, TT), TT, s_g1, 0)
                    exponents()
                turn = turns(s, following)
                for i in range(QT * R):
                    if i == turn["maxima"] + 1 and s >= 1:
                        dve.wait_ge(b_mt, b * NG + s)
                        v.tensor_tensor(qm[(s - 1) % 2], psum[:, 0, :], qs[(s - 1) % 2].bitcast(f32),
                                        ALU.add).then_inc(b_qm, 1)
                        if not front:
                            comparisons()
                            weights()
                    if front:
                        dve.wait_ge(b_sn, b * NP + (s * QT * R + i + 1))
                        v.reduce_max(mx[:, s % 2, i:i + 1], psum[:, 1 + i % 2, :], AX.X).then_inc(b_mx, 1)
                    if s == NG + 1 and i == turn["values"] + 1:
                        values_by_key(b + 1, psum[:, 0, :])
                    if following and i == turn["project"] + 2 and s == NG - 1:
                        compact(2, b + 1, psum[:, 0, :])
                    if i == turn["outputs"] + 1 and s >= 2:
                        normalise(b, s - 2)
                if front:
                    dve.wait_ge(b_mx, b * NP + (s + 1) * QT * R)
                    if s >= 1:
                        dve.wait_ge(b_mt, b * NG + s)
                    m = mx[:, s % 2, :].unsqueeze(2)
                    z = mz[:].rearrange("p t r c -> p (t r) c")
                    v.tensor_scalar(z[:, :, 24:25], m, -1.0, None, ALU.mult).then_inc(b_m1, 1)
                    dve.wait_ge(b_m1, b * NG + (s + 1))
                    v.scalar_tensor_tensor(out=z[:, :, 25:26], in0=m, scalar=-1.0, in1=z[:, :, 24:25].bitcast(f32),
                                           op0=ALU.mult, op1=ALU.subtract).then_inc(b_m2, 1)
                if following and s in (NG - 3, NG - 2):
                    compact(s - (NG - 3), b + 1, psum[:, 0, :])

            compact(2, 0, psum[:, 0, :], 0)
            compact(0, 0, psum[:, 2, :], 1)
            clear()
            compact(1, 0, psum[:, 1, :], 2)
            v.memset(rec[:], 0.0).then_inc(b_on, 1)
            values_by_key(0, psum[:, 3, :])
            low_parts(1, B - 2)
            low_parts(1, B - 1)
            stage(0, 0, False)
            take_logits(1, E1)
            stage(0, 1, False)
            with dve.Fori(0, B - 1) as b:
                for s in range(2, NG + 2):
                    stage(b, s, False)
            for s in range(2, NG + 1):
                stage(B - 1, s, True)
            normalise(B - 1, NG - 1)
            for n in range(2 * B):
                dve.wait_ge(b_nh, n + 1)
                b, k = n // KH, n % KH
                v.tensor_tensor(on_lo[:, k, b * S:(b + 1) * S], psum[:, n, :], on_hi[:, k, b * S:(b + 1) * S].bitcast(f32),
                                ALU.subtract).then_inc(b_nl, 1)
            dve.wait_ge(s_xb, 2)
            for b in range(B):
                dve.wait_ge(b_o, b + 1)
                add_to_tokens(slice(b * QT, (b + 1) * QT), 2 * b).then_inc(b_y, 1)
            feed_forward(1, NF1, G1)


def kernel(**inputs):
    import numpy as np
    import concourse.bacc as bacc
    from concourse.bass_utils import run_bass_kernel_spmd

    a = {k: np.ascontiguousarray(v) for k, v in inputs.items()}
    zeros = lambda *s: np.zeros(s, np.float32)

    def halves(w):
        return w.reshape(KH, P, -1).transpose(1, 0, 2).reshape(P, -1)

    def columns(vec):
        return vec.reshape(-1, P).T

    aw0 = np.concatenate([halves(a["L0_ffn_gate_weight"].T), halves(a["L0_attn_w_qkv"].T),
                          halves(a["L0_attn_w_out"].T)], 1)
    gate1 = np.concatenate([a["L1_ffn_gate_w"], zeros(H, 1)], 1)
    aw1 = np.concatenate([halves(gate1), halves(a["L1_attn_w_qkv"].T), halves(a["L1_attn_w_out"].T)], 1)

    def ffn(gate, up, down, groups, nf, hidden_expert, experts):
        tiles = groups * nf
        out = zeros(groups, P, nf, WS)
        for n in range(tiles):
            g, f = n // nf, n % nf
            c = slice(n * P, (n + 1) * P)
            out[g, :, f, 0:KH * P] = halves(gate[:, c])
            out[g, :, f, KH * P:WC] = halves(up[:, c])
            out[g, :, f, WC:WT] = down[c]
            for r in range(P):
                e = hidden_expert(n * P + r)
                out[g, e, f, WT + r] = 1.0
                out[g, experts + 1 + e, f, WT + r] = 1.0
        return out.reshape(groups * P, nf * WS)

    def wide(w):
        return w.transpose(1, 0, 2).reshape(H, -1)

    pad = G0 * NF0 * P - E0 * F0 - FS0
    ffn0 = ffn(np.concatenate([wide(a["L0_ffn_w_gate"]), a["L0_ffn_ws_gate"], zeros(H, pad)], 1),
               np.concatenate([wide(a["L0_ffn_w_up"]), a["L0_ffn_ws_up"], zeros(H, pad)], 1),
               np.concatenate([a["L0_ffn_w_down"].reshape(-1, H), a["L0_ffn_ws_down"], zeros(pad, H)], 0),
               G0, NF0, lambda i: min(i // F0, E0), E0)
    ffn1 = ffn(np.concatenate([wide(a["L1_ffn_W1"]), a["L1_ffn_Ws1"]], 1),
               np.concatenate([wide(a["L1_ffn_Wg"]), a["L1_ffn_Wsg"]], 1),
               np.concatenate([a["L1_ffn_W2"].reshape(-1, H), a["L1_ffn_Ws2"]], 0),
               G1, NF1, lambda i: i // F1, E1)

    selq, selk = zeros(P, 2, 4, P), zeros(P, 2, NG, P)
    for r in range(R):
        for d in range(HD):
            for slot, part in enumerate((0, 0, 1)):
                for j in range(4):
                    selq[j * 32 + r * HD + d, part, j, 32 * r + slot * HD + d] = 1.0
            for slot, part in enumerate((0, 1, 0)):
                for g in range(NG):
                    selk[g * HD + d, part, g, 32 * r + slot * HD + d] = 1.0
    sel = np.concatenate([selq.reshape(P, -1), selk.reshape(P, -1)], 1)
    const = zeros(P, CF)
    const[:, 0:P] = np.eye(P, dtype=np.float32)
    for r in range(R):
        const[32 * r:32 * r + 32, CF - R + r] = 1.0
        const[32 * r + 3 * HD:32 * r + 3 * HD + 2, P] = 1.0
    for e in range(E0):
        const[:, P + 1 + e * E0:P + 1 + e * E0 + e] = 1.0
    for e in range(E1):
        const[:, P + 1 + E0 * E0 + e * E1:P + 1 + E0 * E0 + e * E1 + e] = 1.0
    bias = np.concatenate([columns(a["L0_attn_b_qkv"]), columns(a["L1_attn_b_qkv"]),
                           np.broadcast_to(a["L1_ffn_gate_b"], (P, E1)),
                           np.broadcast_to(a["L1_ffn_biases"], (P, E1)),
                           np.broadcast_to(a["L0_attn_b_out"], (P, H)),
                           np.broadcast_to(a["L1_attn_b_out"], (P, H))], 1)

    host = {"x": a["L0_attn_hidden_states"].reshape(T, H), "aw0": aw0, "aw1": aw1, "sel": sel,
            "ffn0": ffn0, "ffn1": ffn1, "const": const, "bias": bias}
    nc = bacc.Bacc("TRN2", target_bir_lowering=False, num_devices=1)
    arrays, args = {}, []
    for name, value in host.items():
        arrays[f"in_{name}"] = np.ascontiguousarray(value)
        args.append(nc.dram_tensor(f"in_{name}", value.shape, mybir.dt.float32, kind="ExternalInput").ap())
    args.append(nc.dram_tensor("out_0", (T, H), mybir.dt.float32, kind="ExternalOutput").ap())
    program(nc, *args)
    r = run_bass_kernel_spmd(nc, [arrays], core_ids=[0])
    return r.results[0]["out_0"].reshape(B, S, H)
```
